# Optimizing a Trainium2 kernel written in Bass

```python
import numpy as np
import jax
import jax.numpy as jnp

def _softmax(x, axis=-1):
    return jax.nn.softmax(x, axis=axis)

def _gelu(x):
    return jax.nn.gelu(x, approximate=True)

def _silu(x):
    return jax.nn.silu(x)

def _sigmoid(x):
    return jax.nn.sigmoid(x)

def _layernorm(x, axis=-1, eps=1e-05):
    m = jnp.mean(x, axis=axis, keepdims=True)
    v = jnp.var(x, axis=axis, keepdims=True)
    return (x - m) / jnp.sqrt(v + eps)

def _scatter_add(tgt, idx, src, axis=0):
    return tgt.at[idx].add(src)

def _segment_sum(src, seg, n):
    return jax.ops.segment_sum(src, seg, n)
kernel_name = 'mk_flamingo_gated_d4_seqx_r4_6582ab'

def setup_inputs(seed: int=0):
    np.random.seed(seed)
    _w = jnp.asarray

    def _rec_inputs():
        import jax
        import jax.numpy as jnp
        _rk = jax.random.key(seed)
        x = 0.002226 + 0.9996 * jax.random.normal(jax.random.fold_in(_rk, 1), (16, 256, 256), jnp.float32)
        _lenS = 256 - jax.random.randint(jax.random.fold_in(_rk, 7), (16,), 0, max(1, 256 // 4) + 1, jnp.int32)
        _lenS2 = 256 - jax.random.randint(jax.random.fold_in(_rk, 8), (16,), 0, max(1, 256 // 4) + 1, jnp.int32)
        _ctx_1024P = jax.random.normal(jax.random.fold_in(_rk, 11), (16, 16, 256), jnp.float32)
        _ctx_1024c = jax.random.dirichlet(jax.random.fold_in(_rk, 511), 0.3 * jnp.ones((16,), jnp.float32), (16, 256))
        _ctx_1024t = jnp.einsum('bsk,bkd->bsd', _ctx_1024c, _ctx_1024P)
        _ctx_1024t = _ctx_1024t * jax.lax.rsqrt(jnp.mean(jnp.square(_ctx_1024t)) + 1e-12) * 0.953939
        ctx_1024 = -0.000125008 + 0.999885 * (_ctx_1024t + 0.3 * jax.random.normal(jax.random.fold_in(_rk, 611), (16, 256, 256), jnp.float32))
        _validS = jnp.arange(256)[None, :] < _lenS[:, None]
        _validS2 = jnp.arange(256)[None, :] < _lenS2[:, None]
        _causal = jnp.tril(jnp.ones((256, 256), dtype=bool))
        mask_BxS2_bk0 = jnp.logical_not(jnp.broadcast_to(_validS2[:, :], (16, 256)))
        mask_1x1xSxS2_ik0 = jnp.where(jnp.broadcast_to(_validS2[0:1, None, None, :], (1, 1, 256, 256)), 0, 1).astype(jnp.int32)
        _g = jax.random.normal(jax.random.fold_in(_rk, 9001), (2, 4), jnp.float32)
        _g = jnp.sign(_g) * jnp.maximum(jnp.abs(_g), 1.0) + (_g == 0) * 1.0
        g_xattn = _g[0]
        g_ffn = _g[1]
        return (x, ctx_1024, mask_BxS2_bk0, mask_1x1xSxS2_ik0, g_xattn, g_ffn)
    x, ctx_1024, mask_BxS2_bk0, mask_1x1xSxS2_ik0, g_xattn, g_ffn = _rec_inputs()

    def _L0_xattn_setup():
        import jax, jax.numpy as jnp
        import numpy as np
        DIM = 256
        HEADS = 16
        DIM_HEAD = 64
        INNER = HEADS * DIM_HEAD
        EPS = 1e-05

        def layernorm(t, g, b):
            mu = jnp.mean(t, axis=-1, keepdims=True)
            var = jnp.var(t, axis=-1, keepdims=True)
            return (t - mu) * jax.lax.rsqrt(var + EPS) * g + b
        key = jax.random.key(seed)
        ks = jax.random.split(key, 8)
        b, n, m = (8, 1024, 64)
        x = jax.random.normal(ks[0], (b, n, DIM), dtype=jnp.float32)
        latents = jax.random.normal(ks[1], (b, m, DIM), dtype=jnp.float32)
        mask = jax.random.randint(ks[2], (b, n), 0, 2).astype(bool)
        s = 0.02
        Wq = jax.random.normal(ks[3], (DIM, INNER), dtype=jnp.float32) * s
        Wkv = jax.random.normal(ks[4], (DIM, 2 * INNER), dtype=jnp.float32) * s
        Wout = jax.random.normal(ks[5], (INNER, DIM), dtype=jnp.float32) * s
        ln_x_g = jnp.ones((DIM,), jnp.float32)
        ln_x_b = jnp.zeros((DIM,), jnp.float32)
        ln_l_g = jnp.ones((DIM,), jnp.float32)
        ln_l_b = jnp.zeros((DIM,), jnp.float32)
        ln_o_g = jnp.ones((DIM,), jnp.float32)
        ln_o_b = jnp.zeros((DIM,), jnp.float32)
        return {'x': x, 'latents': latents, 'mask': mask, 'ln_x_g': ln_x_g, 'ln_x_b': ln_x_b, 'ln_l_g': ln_l_g, 'ln_l_b': ln_l_b, 'Wq': Wq, 'Wkv': Wkv, 'Wout': Wout, 'ln_o_g': ln_o_g, 'ln_o_b': ln_o_b}
    _L0_xattn_all = _L0_xattn_setup()
    _L0_xattn_in = {k: v for k, v in _L0_xattn_all.items() if k in ('ln_x_g', 'ln_x_b', 'ln_l_g', 'ln_l_b', 'Wq', 'Wkv', 'Wout', 'ln_o_g', 'ln_o_b')}
    del _L0_xattn_all

    def _L0_ffn_setup():
        import jax, jax.numpy as jnp
        import numpy as np
        import math
        DIM = 256
        NUM_HEADS = 16
        SHARED_HEADS = 1
        ROUTED_HEADS = 3
        HEAD_DIM = DIM // NUM_HEADS
        B, N = (2, 512)
        key = jax.random.key(seed)
        ks = jax.random.split(key, 16)
        s = 1.0 / math.sqrt(DIM)
        inp = {'x': jax.random.normal(ks[0], (B, N, DIM), dtype=jnp.float32), 'Wq': jax.random.uniform(ks[1], (DIM, DIM), minval=-s, maxval=s), 'bq': jax.random.uniform(ks[2], (DIM,), minval=-s, maxval=s), 'Wk': jax.random.uniform(ks[3], (DIM, DIM), minval=-s, maxval=s), 'bk': jax.random.uniform(ks[4], (DIM,), minval=-s, maxval=s), 'Wv': jax.random.uniform(ks[5], (DIM, DIM), minval=-s, maxval=s), 'bv': jax.random.uniform(ks[6], (DIM,), minval=-s, maxval=s), 'Wp': jax.random.uniform(ks[7], (DIM, DIM), minval=-s, maxval=s), 'bp': jax.random.uniform(ks[8], (DIM,), minval=-s, maxval=s), 'Wr': jax.random.uniform(ks[9], (NUM_HEADS - SHARED_HEADS, DIM), minval=-s, maxval=s), 'br': jax.random.uniform(ks[10], (NUM_HEADS - SHARED_HEADS,), minval=-s, maxval=s), 'Ws': jax.random.uniform(ks[11], (2, DIM), minval=-s, maxval=s), 'bs': jax.random.uniform(ks[12], (2,), minval=-s, maxval=s), 'temperature': jnp.full((NUM_HEADS, 1, 1), float(np.log(np.expm1(1.0 / 0.24))), dtype=jnp.float32), 'query_embedding': 0.02 * jax.random.normal(ks[13], (NUM_HEADS, 1, HEAD_DIM), dtype=jnp.float32)}
        return inp
    _L0_ffn_all = _L0_ffn_setup()
    _L0_ffn_in = {k: v for k, v in _L0_ffn_all.items() if k in ('Wq', 'bq', 'Wk', 'bk', 'Wv', 'bv', 'Wp', 'bp', 'Wr', 'br', 'Ws', 'bs', 'temperature', 'query_embedding')}
    del _L0_ffn_all

    def _L1_xattn_setup():
        import jax, jax.numpy as jnp
        import numpy as np
        key = jax.random.key(seed)
        k1, k2, k3 = jax.random.split(key, 3)
        B, N_LAT, N_CTX, D_MODEL = (2, 256, 1024, 256)
        x = jax.random.normal(k1, (B, N_LAT, D_MODEL), dtype=jnp.float32)
        context = jax.random.normal(k2, (B, N_CTX, D_MODEL), dtype=jnp.float32)
        W_out = jax.random.normal(k3, (D_MODEL, D_MODEL), dtype=jnp.float32) * D_MODEL ** (-0.5)
        b_out = jnp.zeros((D_MODEL,), dtype=jnp.float32)
        return {'x': x, 'context': context, 'W_out': W_out, 'b_out': b_out, 'heads': 16}
    _L1_xattn_all = _L1_xattn_setup()
    _L1_xattn_in = {k: v for k, v in _L1_xattn_all.items() if k in ('W_out', 'b_out')}
    del _L1_xattn_all

    def _L1_ffn_setup():
        import jax, jax.numpy as jnp
        import numpy as np
        H = 256
        I = 512
        E = 32
        B, S = (4, 512)

        def _grouped_mm(a, w, group_sizes):
            return jax.lax.ragged_dot(a, w, group_sizes)

        def _swiglu(x, gw, uw, dw):
            return jax.nn.silu(x @ gw) * (x @ uw) @ dw
        key = jax.random.key(seed)
        ks = jax.random.split(key, 8)
        scale = 0.02
        inp = {'hidden_states': jax.random.normal(ks[0], (B, S, H), dtype=jnp.float32), 'gate_w': jax.random.normal(ks[1], (H, E), dtype=jnp.float32) * scale, 'shared_gate_w': jax.random.normal(ks[2], (H, I), dtype=jnp.float32) * scale, 'shared_up_w': jax.random.normal(ks[3], (H, I), dtype=jnp.float32) * scale, 'shared_down_w': jax.random.normal(ks[4], (I, H), dtype=jnp.float32) * scale, 'routed_gate_w': jax.random.normal(ks[5], (E, H, I), dtype=jnp.float32) * scale, 'routed_up_w': jax.random.normal(ks[6], (E, H, I), dtype=jnp.float32) * scale, 'routed_down_w': jax.random.normal(ks[7], (E, I, H), dtype=jnp.float32) * scale}
        return inp
    _L1_ffn_all = _L1_ffn_setup()
    _L1_ffn_in = {k: v for k, v in _L1_ffn_all.items() if k in ('gate_w', 'shared_gate_w', 'shared_up_w', 'shared_down_w', 'routed_gate_w', 'routed_up_w', 'routed_down_w')}
    del _L1_ffn_all

    def _L2_xattn_setup():
        import jax, jax.numpy as jnp
        import numpy as np
        B, L_ENC, L_DEC, D = (16, 128, 128, 256)
        key = jax.random.key(seed)
        k1, k2, k3, k4, k5, k6 = jax.random.split(key, 6)
        encoder_hc = jax.random.normal(k1, (B, L_ENC, D), dtype=jnp.float32)
        decoder_hq = jax.random.normal(k2, (B, L_DEC, D), dtype=jnp.float32)
        w_sim = jax.random.normal(k3, (3 * D,), dtype=jnp.float32) * 0.02
        b_sim = jax.random.normal(k4, (1,), dtype=jnp.float32) * 0.02
        W_qv = jax.random.normal(k5, (4 * D, D), dtype=jnp.float32) * 0.02
        b_qv = jax.random.normal(k6, (D,), dtype=jnp.float32) * 0.02
        return {'encoder_hc': encoder_hc, 'decoder_hq': decoder_hq, 'w_sim': w_sim, 'b_sim': b_sim, 'W_qv': W_qv, 'b_qv': b_qv}
    _L2_xattn_all = _L2_xattn_setup()
    _L2_xattn_in = {k: v for k, v in _L2_xattn_all.items() if k in ('w_sim', 'b_sim', 'W_qv', 'b_qv')}
    del _L2_xattn_all

    def _L2_ffn_setup():
        import jax, jax.numpy as jnp
        import numpy as np
        D_MODEL = 256
        M = 64
        INNER = 16
        key = jax.random.key(seed)
        ks = jax.random.split(key, 9)

        def init(k, shape, fan_in):
            bound = 1.0 / np.sqrt(fan_in)
            return jax.random.uniform(k, shape, jnp.float32, -bound, bound)
        x = jax.random.normal(ks[0], (16, 1024, D_MODEL), dtype=jnp.float32)
        Win = init(ks[1], (D_MODEL, M), D_MODEL)
        bin_ = init(ks[2], (M,), D_MODEL)
        W1 = init(ks[3], (M, INNER), 1)
        b1 = init(ks[4], (M, INNER), 1)
        W2 = init(ks[5], (M, INNER), INNER)
        b2 = init(ks[6], (M,), INNER)
        Wout = init(ks[7], (M, D_MODEL), M)
        bout = init(ks[8], (D_MODEL,), M)
        return {'x': x, 'Win': Win, 'bin_': bin_, 'W1': W1, 'b1': b1, 'W2': W2, 'b2': b2, 'Wout': Wout, 'bout': bout}
    _L2_ffn_all = _L2_ffn_setup()
    _L2_ffn_in = {k: v for k, v in _L2_ffn_all.items() if k in ('Win', 'bin_', 'W1', 'b1', 'W2', 'b2', 'Wout', 'bout')}
    del _L2_ffn_all

    def _L3_xattn_setup():
        import jax, jax.numpy as jnp
        import numpy as np
        import math
        EMBED = 256
        HEADS = 16
        HEAD_DIM = EMBED // HEADS
        WINDOW = 128
        B, S = (2, 512)
        key = jax.random.key(seed)
        k1, k2, k3, k4 = jax.random.split(key, 4)
        values = jax.random.normal(k1, (B, S, EMBED), dtype=jnp.float32)
        keys = jax.random.normal(k2, (B, S, EMBED), dtype=jnp.float32)
        queries = jax.random.normal(k3, (B, S, EMBED), dtype=jnp.float32)
        idx = jnp.arange(S)
        band = (jnp.abs(idx[:, None] - idx[None, :]) <= WINDOW // 2).astype(jnp.int32)
        mask = band[None, None, :, :]
        w_out = jax.random.normal(k4, (EMBED, EMBED), dtype=jnp.float32) * (1.0 / math.sqrt(EMBED))
        b_out = jnp.zeros((EMBED,), dtype=jnp.float32)
        return {'values': values, 'keys': keys, 'queries': queries, 'mask': mask, 'w_out': w_out, 'b_out': b_out}
    _L3_xattn_all = _L3_xattn_setup()
    _L3_xattn_in = {k: v for k, v in _L3_xattn_all.items() if k in ('w_out', 'b_out')}
    del _L3_xattn_all

    def _L3_ffn_setup():
        import jax, jax.numpy as jnp
        import numpy as np
        TOPK = 4
        key = jax.random.key(seed)
        ks = jax.random.split(key, 9)
        B, T, D = (4, 512, 256)
        E, H = (32, 128)
        HS = H * TOPK
        s = lambda k, shape, fan: jax.random.normal(k, shape, dtype=jnp.float32) / np.sqrt(fan)
        return {'x': jax.random.normal(ks[0], (B, T, D), dtype=jnp.float32), 'router_w': s(ks[1], (E, D), D), 'router_bias': jnp.zeros((E,), dtype=jnp.float32), 'gate_w': s(ks[2], (E, H, D), D), 'up_w': s(ks[3], (E, H, D), D), 'down_w': s(ks[4], (E, D, H), H), 'sgate_w': s(ks[5], (HS, D), D), 'sup_w': s(ks[6], (HS, D), D), 'sdown_w': s(ks[7], (D, HS), HS)}
    _L3_ffn_all = _L3_ffn_setup()
    _L3_ffn_in = {k: v for k, v in _L3_ffn_all.items() if k in ('router_w', 'router_bias', 'gate_w', 'up_w', 'down_w', 'sgate_w', 'sup_w', 'sdown_w')}
    del _L3_ffn_all
    return {'x': x, 'ctx_1024': ctx_1024, 'mask_BxS2_bk0': mask_BxS2_bk0, 'mask_1x1xSxS2_ik0': mask_1x1xSxS2_ik0, 'g_xattn': g_xattn, 'g_ffn': g_ffn, 'L0_xattn_ln_x_g': _L0_xattn_in['ln_x_g'], 'L0_xattn_ln_x_b': _L0_xattn_in['ln_x_b'], 'L0_xattn_ln_l_g': _L0_xattn_in['ln_l_g'], 'L0_xattn_ln_l_b': _L0_xattn_in['ln_l_b'], 'L0_xattn_Wq': _L0_xattn_in['Wq'], 'L0_xattn_Wkv': _L0_xattn_in['Wkv'], 'L0_xattn_Wout': _L0_xattn_in['Wout'], 'L0_xattn_ln_o_g': _L0_xattn_in['ln_o_g'], 'L0_xattn_ln_o_b': _L0_xattn_in['ln_o_b'], 'L0_ffn_Wq': _L0_ffn_in['Wq'], 'L0_ffn_bq': _L0_ffn_in['bq'], 'L0_ffn_Wk': _L0_ffn_in['Wk'], 'L0_ffn_bk': _L0_ffn_in['bk'], 'L0_ffn_Wv': _L0_ffn_in['Wv'], 'L0_ffn_bv': _L0_ffn_in['bv'], 'L0_ffn_Wp': _L0_ffn_in['Wp'], 'L0_ffn_bp': _L0_ffn_in['bp'], 'L0_ffn_Wr': _L0_ffn_in['Wr'], 'L0_ffn_br': _L0_ffn_in['br'], 'L0_ffn_Ws': _L0_ffn_in['Ws'], 'L0_ffn_bs': _L0_ffn_in['bs'], 'L0_ffn_temperature': _L0_ffn_in['temperature'], 'L0_ffn_query_embedding': _L0_ffn_in['query_embedding'], 'L1_xattn_W_out': _L1_xattn_in['W_out'], 'L1_xattn_b_out': _L1_xattn_in['b_out'], 'L1_ffn_gate_w': _L1_ffn_in['gate_w'], 'L1_ffn_shared_gate_w': _L1_ffn_in['shared_gate_w'], 'L1_ffn_shared_up_w': _L1_ffn_in['shared_up_w'], 'L1_ffn_shared_down_w': _L1_ffn_in['shared_down_w'], 'L1_ffn_routed_gate_w': _L1_ffn_in['routed_gate_w'], 'L1_ffn_routed_up_w': _L1_ffn_in['routed_up_w'], 'L1_ffn_routed_down_w': _L1_ffn_in['routed_down_w'], 'L2_xattn_w_sim': _L2_xattn_in['w_sim'], 'L2_xattn_b_sim': _L2_xattn_in['b_sim'], 'L2_xattn_W_qv': _L2_xattn_in['W_qv'], 'L2_xattn_b_qv': _L2_xattn_in['b_qv'], 'L2_ffn_Win': _L2_ffn_in['Win'], 'L2_ffn_bin_': _L2_ffn_in['bin_'], 'L2_ffn_W1': _L2_ffn_in['W1'], 'L2_ffn_b1': _L2_ffn_in['b1'], 'L2_ffn_W2': _L2_ffn_in['W2'], 'L2_ffn_b2': _L2_ffn_in['b2'], 'L2_ffn_Wout': _L2_ffn_in['Wout'], 'L2_ffn_bout': _L2_ffn_in['bout'], 'L3_xattn_w_out': _L3_xattn_in['w_out'], 'L3_xattn_b_out': _L3_xattn_in['b_out'], 'L3_ffn_router_w': _L3_ffn_in['router_w'], 'L3_ffn_router_bias': _L3_ffn_in['router_bias'], 'L3_ffn_gate_w': _L3_ffn_in['gate_w'], 'L3_ffn_up_w': _L3_ffn_in['up_w'], 'L3_ffn_down_w': _L3_ffn_in['down_w'], 'L3_ffn_sgate_w': _L3_ffn_in['sgate_w'], 'L3_ffn_sup_w': _L3_ffn_in['sup_w'], 'L3_ffn_sdown_w': _L3_ffn_in['sdown_w']}

def reference(x, ctx_1024, mask_BxS2_bk0, mask_1x1xSxS2_ik0, g_xattn, g_ffn, L0_xattn_ln_x_g, L0_xattn_ln_x_b, L0_xattn_ln_l_g, L0_xattn_ln_l_b, L0_xattn_Wq, L0_xattn_Wkv, L0_xattn_Wout, L0_xattn_ln_o_g, L0_xattn_ln_o_b, L0_ffn_Wq, L0_ffn_bq, L0_ffn_Wk, L0_ffn_bk, L0_ffn_Wv, L0_ffn_bv, L0_ffn_Wp, L0_ffn_bp, L0_ffn_Wr, L0_ffn_br, L0_ffn_Ws, L0_ffn_bs, L0_ffn_temperature, L0_ffn_query_embedding, L1_xattn_W_out, L1_xattn_b_out, L1_ffn_gate_w, L1_ffn_shared_gate_w, L1_ffn_shared_up_w, L1_ffn_shared_down_w, L1_ffn_routed_gate_w, L1_ffn_routed_up_w, L1_ffn_routed_down_w, L2_xattn_w_sim, L2_xattn_b_sim, L2_xattn_W_qv, L2_xattn_b_qv, L2_ffn_Win, L2_ffn_bin_, L2_ffn_W1, L2_ffn_b1, L2_ffn_W2, L2_ffn_b2, L2_ffn_Wout, L2_ffn_bout, L3_xattn_w_out, L3_xattn_b_out, L3_ffn_router_w, L3_ffn_router_bias, L3_ffn_gate_w, L3_ffn_up_w, L3_ffn_down_w, L3_ffn_sgate_w, L3_ffn_sup_w, L3_ffn_sdown_w):
    import jax
    import jax.numpy as jnp

    def _L0_xattn_ref(x, latents, mask, ln_x_g, ln_x_b, ln_l_g, ln_l_b, Wq, Wkv, Wout, ln_o_g, ln_o_b):
        import jax, jax.numpy as jnp
        import numpy as np
        DIM = 256
        HEADS = 16
        DIM_HEAD = 64
        INNER = HEADS * DIM_HEAD
        EPS = 1e-05

        def layernorm(t, g, b):
            mu = jnp.mean(t, axis=-1, keepdims=True)
            var = jnp.var(t, axis=-1, keepdims=True)
            return (t - mu) * jax.lax.rsqrt(var + EPS) * g + b
        b, n, _ = x.shape
        m = latents.shape[1]
        scale = DIM_HEAD ** (-0.5)
        xn = layernorm(x, ln_x_g, ln_x_b)
        ln = layernorm(latents, ln_l_g, ln_l_b)
        q = ln @ Wq
        kv_input = jnp.concatenate((xn, ln), axis=1)
        kv = kv_input @ Wkv
        k, v = jnp.split(kv, 2, axis=-1)

        def heads(t):
            return t.reshape(t.shape[0], t.shape[1], HEADS, DIM_HEAD).transpose(0, 2, 1, 3)
        q, k, v = (heads(q) * scale, heads(k), heads(v))
        sim = jnp.einsum('bhid,bhjd->bhij', q, k)
        mask_full = jnp.concatenate((mask, jnp.ones((b, m), dtype=bool)), axis=1)
        max_neg = -jnp.finfo(sim.dtype).max
        sim = jnp.where(mask_full[:, None, None, :], sim, max_neg)
        attn = jax.nn.softmax(sim.astype(jnp.float32), axis=-1).astype(sim.dtype)
        out = jnp.einsum('bhij,bhjd->bhid', attn, v)
        out = out.transpose(0, 2, 1, 3).reshape(b, m, INNER)
        out = out @ Wout
        return layernorm(out, ln_o_g, ln_o_b)

    def _L0_ffn_ref(x, Wq, bq, Wk, bk, Wv, bv, Wp, bp, Wr, br, Ws, bs, temperature, query_embedding):
        import jax, jax.numpy as jnp
        import numpy as np
        import math
        DIM = 256
        NUM_HEADS = 16
        SHARED_HEADS = 1
        ROUTED_HEADS = 3
        HEAD_DIM = DIM // NUM_HEADS
        B, N = (2, 512)
        Bsz, Nn, C = x.shape
        H, hd = (NUM_HEADS, HEAD_DIM)

        def heads(W, b):
            y = x @ W.T + b
            return y.reshape(Bsz, Nn, H, hd).transpose(0, 2, 1, 3)
        q = heads(Wq, bq)
        k = heads(Wk, bk)
        v = heads(Wv, bv)
        q_norm = q / jnp.linalg.norm(q, axis=-1, keepdims=True)
        q_scaled = (q_norm + query_embedding[None]) * jax.nn.softplus(temperature)[None]
        attn = jnp.einsum('bhqd,bhkd->bhqk', q_scaled, k) / math.sqrt(hd)
        attn = jax.nn.softmax(attn, axis=-1)
        h = jnp.einsum('bhqk,bhkd->bhqd', attn, v)
        h = h.transpose(0, 2, 1, 3).reshape(Bsz, Nn, C)
        gates = jax.nn.softmax(h @ Wr.T + br, axis=-1)
        _, idx = jax.lax.top_k(gates, ROUTED_HEADS)
        mask = jax.nn.one_hot(idx, H - SHARED_HEADS, dtype=gates.dtype).sum(axis=-2)
        routed_gates = gates * mask * ROUTED_HEADS
        sw = jax.nn.softmax(h @ Ws.T + bs, axis=-1)
        shared_gates = sw * SHARED_HEADS
        weight_0 = sw * 2.0
        shared_gates = weight_0[..., 0:1] * shared_gates
        routed_gates = weight_0[..., 1:2] * routed_gates
        masked_gates = jnp.concatenate([shared_gates, routed_gates], axis=-1)
        out = h * masked_gates.sum(axis=-1, keepdims=True)
        return out @ Wp.T + bp

    def _L1_xattn_ref(x, context, W_out, b_out, heads):
        import jax, jax.numpy as jnp
        import numpy as np
        b, i, dm = x.shape
        j = context.shape[1]
        d = dm // heads
        scale = d ** (-0.5)
        q = x.reshape(b, i, heads, d).transpose(0, 2, 1, 3)
        k = context.reshape(b, j, heads, d).transpose(0, 2, 1, 3)
        v = k
        sim = jnp.einsum('bhid,bhjd->bhij', q, k) * scale
        attn = jax.nn.softmax(sim, axis=-1)
        out = jnp.einsum('bhij,bhjd->bhid', attn, v)
        out = out.transpose(0, 2, 1, 3).reshape(b, i, dm)
        return out @ W_out.T + b_out

    def _L1_ffn_ref(hidden_states, gate_w, shared_gate_w, shared_up_w, shared_down_w, routed_gate_w, routed_up_w, routed_down_w):
        import jax, jax.numpy as jnp
        import numpy as np
        H = 256
        I = 512
        E = 32
        B, S = (4, 512)

        def _grouped_mm(a, w, group_sizes):
            return jax.lax.ragged_dot(a, w, group_sizes)

        def _swiglu(x, gw, uw, dw):
            return jax.nn.silu(x @ gw) * (x @ uw) @ dw
        b, s, h = hidden_states.shape
        x = hidden_states.reshape(-1, h)
        shared_out = _swiglu(x, shared_gate_w, shared_up_w, shared_down_w)
        logits = x @ gate_w
        topk_ids = jnp.argmax(logits, axis=-1)
        topk_val = jnp.max(logits, axis=-1)
        scores = jax.nn.sigmoid(topk_val)[:, None]
        xs = x * scores
        tokens_per_expert = jnp.zeros((E,), jnp.int32).at[topk_ids].add(1)
        order = jnp.argsort(topk_ids)
        sorted_x = xs[order]
        g = _grouped_mm(sorted_x, routed_gate_w, tokens_per_expert)
        u = _grouped_mm(sorted_x, routed_up_w, tokens_per_expert)
        d = _grouped_mm(jax.nn.silu(g) * u, routed_down_w, tokens_per_expert)
        inv = jnp.argsort(order)
        routed_out = d[inv]
        return (shared_out + routed_out).reshape(b, s, h)

    def _L2_xattn_ref(encoder_hc, decoder_hq, w_sim, b_sim, W_qv, b_qv):
        import jax, jax.numpy as jnp
        import numpy as np
        B, L_ENC, L_DEC, D = (16, 128, 128, 256)
        d = encoder_hc.shape[-1]
        w1, w2, w3 = (w_sim[:d], w_sim[d:2 * d], w_sim[2 * d:])
        Sim = (encoder_hc @ w1)[:, :, None] + (decoder_hq @ w2)[:, None, :] + jnp.einsum('bid,bjd->bij', encoder_hc * w3, decoder_hq) + b_sim[0]
        A = jax.nn.softmax(Sim, axis=2)
        hq_hat = jnp.einsum('bij,bjd->bid', A, decoder_hq)
        Batt = jax.nn.softmax(jnp.max(Sim, axis=2), axis=1)
        hc_bar = jnp.einsum('bi,bid->bd', Batt, encoder_hc)[:, None, :]
        hc_hat = jnp.broadcast_to(hc_bar, encoder_hc.shape)
        feats = jnp.concatenate([encoder_hc, hq_hat, encoder_hc * hq_hat, encoder_hc * hc_hat], axis=-1)
        hcq = feats @ W_qv + b_qv
        return hcq

    def _L2_ffn_ref(x, Win, bin_, W1, b1, W2, b2, Wout, bout):
        import jax, jax.numpy as jnp
        import numpy as np
        D_MODEL = 256
        M = 64
        INNER = 16
        s = jnp.einsum('btd,dm->btm', x, Win) + bin_
        h = jax.nn.relu(s[..., None] * W1 + b1)
        g = jnp.einsum('btmh,mh->btm', h, W2) + b2
        out = jnp.einsum('btm,md->btd', g, Wout) + bout
        return out

    def _L3_xattn_ref(values, keys, queries, mask, w_out, b_out):
        import jax, jax.numpy as jnp
        import numpy as np
        import math
        EMBED = 256
        HEADS = 16
        HEAD_DIM = EMBED // HEADS
        WINDOW = 128
        B, S = (2, 512)
        N, q_len = (queries.shape[0], queries.shape[1])
        v = values.reshape(N, -1, HEADS, HEAD_DIM)
        k = keys.reshape(N, -1, HEADS, HEAD_DIM)
        q = queries.reshape(N, -1, HEADS, HEAD_DIM)
        energy = jnp.einsum('nqhd,nkhd->nhqk', q, k)
        energy = jnp.where(mask == 0, jnp.float32(-1e+20), energy)
        attn = jax.nn.softmax(energy / math.sqrt(EMBED), axis=3)
        out = jnp.einsum('nhql,nlhd->nqhd', attn, v).reshape(N, q_len, HEADS * HEAD_DIM)
        return out @ w_out.T + b_out

    def _L3_ffn_ref(x, router_w, router_bias, gate_w, up_w, down_w, sgate_w, sup_w, sdown_w):
        import jax, jax.numpy as jnp
        import numpy as np
        TOPK = 4
        B, T, D = x.shape
        flat = x.reshape(B * T, D)
        logits = flat.astype(jnp.float32) @ router_w.T + router_bias
        scores = jax.nn.softmax(logits, axis=-1)
        topk_scores, topk_idx = jax.lax.top_k(scores, TOPK)
        topk_scores = topk_scores / jnp.clip(topk_scores.sum(axis=-1, keepdims=True), 1e-12, None)
        h = jax.nn.silu(jnp.einsum('nd,ehd->neh', flat, gate_w)) * jnp.einsum('nd,ehd->neh', flat, up_w)
        expert_out = jnp.einsum('neh,edh->ned', h, down_w)
        sel = jnp.take_along_axis(expert_out, topk_idx[:, :, None], axis=1)
        out = (sel * topk_scores.astype(flat.dtype)[:, :, None]).sum(axis=1)
        out = out + jax.nn.silu(flat @ sgate_w.T) * (flat @ sup_w.T) @ sdown_w.T
        return out.reshape(B, T, D)
    x = x + jnp.tanh(g_xattn[0]) * _L0_xattn_ref(ctx_1024, _layernorm(x, axis=-1), mask_BxS2_bk0, L0_xattn_ln_x_g, L0_xattn_ln_x_b, L0_xattn_ln_l_g, L0_xattn_ln_l_b, L0_xattn_Wq, L0_xattn_Wkv, L0_xattn_Wout, L0_xattn_ln_o_g, L0_xattn_ln_o_b)
    x = x + jnp.tanh(g_ffn[0]) * _L0_ffn_ref(_layernorm(x, axis=-1), L0_ffn_Wq, L0_ffn_bq, L0_ffn_Wk, L0_ffn_bk, L0_ffn_Wv, L0_ffn_bv, L0_ffn_Wp, L0_ffn_bp, L0_ffn_Wr, L0_ffn_br, L0_ffn_Ws, L0_ffn_bs, L0_ffn_temperature, L0_ffn_query_embedding)
    x = x + jnp.tanh(g_xattn[1]) * _L1_xattn_ref(_layernorm(x, axis=-1), ctx_1024, L1_xattn_W_out, L1_xattn_b_out, 16)
    x = x + jnp.tanh(g_ffn[1]) * _L1_ffn_ref(_layernorm(x, axis=-1), L1_ffn_gate_w, L1_ffn_shared_gate_w, L1_ffn_shared_up_w, L1_ffn_shared_down_w, L1_ffn_routed_gate_w, L1_ffn_routed_up_w, L1_ffn_routed_down_w)
    x = x + jnp.tanh(g_xattn[2]) * _L2_xattn_ref(_layernorm(x, axis=-1), ctx_1024, L2_xattn_w_sim, L2_xattn_b_sim, L2_xattn_W_qv, L2_xattn_b_qv)
    x = x + jnp.tanh(g_ffn[2]) * _L2_ffn_ref(_layernorm(x, axis=-1), L2_ffn_Win, L2_ffn_bin_, L2_ffn_W1, L2_ffn_b1, L2_ffn_W2, L2_ffn_b2, L2_ffn_Wout, L2_ffn_bout)
    x = x + jnp.tanh(g_xattn[3]) * _L3_xattn_ref(ctx_1024, ctx_1024, _layernorm(x, axis=-1), mask_1x1xSxS2_ik0, L3_xattn_w_out, L3_xattn_b_out)
    x = x + jnp.tanh(g_ffn[3]) * _L3_ffn_ref(_layernorm(x, axis=-1), L3_ffn_router_w, L3_ffn_router_bias, L3_ffn_gate_w, L3_ffn_up_w, L3_ffn_down_w, L3_ffn_sgate_w, L3_ffn_sup_w, L3_ffn_sdown_w)
    return x

_drawn_inputs = setup_inputs


def setup_inputs(seed=0):
    import zlib

    import numpy as np

    out = dict(_drawn_inputs(seed))
    spreads = {'L0_xattn_ln_x_g': (1.0, 0.2),
     'L0_xattn_ln_x_b': (0.0, 0.1),
     'L0_xattn_ln_l_g': (1.0, 0.2),
     'L0_xattn_ln_l_b': (0.0, 0.1),
     'L0_xattn_ln_o_g': (1.0, 0.2),
     'L0_xattn_ln_o_b': (0.0, 0.1),
     'L0_ffn_temperature': (4.151041507720947, 0.6),
     'L1_xattn_b_out': (0.0, 0.1),
     'L3_xattn_b_out': (0.0, 0.372),
     'L3_ffn_router_bias': (0.0, 0.366)}
    factors = {'g_ffn': 28.888,
     'L0_ffn_Wq': 3.385,
     'L0_ffn_bq': 8.0,
     'L0_ffn_Wk': 3.339,
     'L0_ffn_bk': 64.0,
     'L0_ffn_Wr': 7.429,
     'L0_ffn_br': 8.0,
     'L0_ffn_Ws': 4.979,
     'L0_ffn_bs': 8.0,
     'L0_ffn_query_embedding': 8.0,
     'L1_ffn_gate_w': 5.31,
     'L1_ffn_shared_gate_w': 2.672,
     'L1_ffn_shared_up_w': 2.713,
     'L1_ffn_shared_down_w': 2.703,
     'L1_ffn_routed_gate_w': 4.898,
     'L1_ffn_routed_up_w': 4.948,
     'L1_ffn_routed_down_w': 5.203,
     'L2_xattn_b_qv': 11.989,
     'L2_ffn_bin_': 44.721,
     'L2_xattn_w_sim': 5.198,
     'L2_ffn_Win': 2.915,
     'L2_ffn_W1': 2.861,
     'L2_ffn_bout': 2.839}
    for name, (base, spread) in spreads.items():
        noise = np.random.default_rng([zlib.crc32(name.encode()), seed]).standard_normal(out[name].shape)
        drawn = base * np.exp(spread * noise) if base else spread * noise
        out[name] = jnp.asarray(drawn.astype(out[name].dtype))
    for name, factor in factors.items():
        out[name] = (out[name] * factor).astype(out[name].dtype)
    return out
```

```python
from contextlib import ExitStack

import concourse.bass as bass
from concourse import mybir

P = 128
F32 = mybir.dt.float32
BF16 = mybir.dt.bfloat16
I32 = mybir.dt.int32
U32 = mybir.dt.uint32
U8 = mybir.dt.uint8
ALU = mybir.AluOpType
ACT = mybir.ActivationFunctionType
AX = mybir.AxisListType

EPS = 1e-5
FLT_MAX = 3.4028234663852886e38
BIG = 99972459978862329856.0
HEADS = 16
HD = 16
SLOT = 32
RING = 3
ACCS = 2


class Rotation:

    def __init__(self, order, slots, full, taken):
        self.n = {name: i for i, name in enumerate(order)}
        assert len(self.n) == len(order)
        self.slots, self.full_sem, self.taken_sem = slots, full, taken

    def slot(self, name):
        return self.n[name] % self.slots

    def full(self, name):
        return self.full_sem[self.slot(name)]

    def taken(self, name):
        return self.taken_sem[self.slot(name)]

    def count(self, name):
        return self.n[name] // self.slots + 1

    def wait_room(self, pe, name):
        if self.count(name) > 1:
            pe.wait_ge(self.taken(name), self.count(name) - 1)

    def wait_full(self, eng, name):
        eng.wait_ge(self.full(name), self.count(name))

    def wait_taken(self, eng, name):
        eng.wait_ge(self.taken(name), self.count(name))


class Stage(ExitStack):

    def __init__(self):
        super().__init__()
        self.used = []


def chain(eng, sem, asked=None, given=None):
    def link(ins):
        link.made += 1
        ins.then_inc(sem, 1)
        eng.wait_ge(sem, link.made)

    link.made = 0
    link.asked, link.root_asked, link.root_given = 0, asked, given
    return link


def narrow_order(tag):
    return ([(tag, "Q", 0), (tag, "Q", 1)] + [(tag, "S", i) for i in range(6)] + [(tag, "Q2", 0)]
            + [(tag, "S", i) for i in range(6, 8)] + [(tag, "T", i) for i in range(2)] + [(tag, "Q2", 1)]
            + [(tag, "T", i) for i in range(2, 8)])


PT_LAG, AV_LAG = 3, 4


def build(nc, a, out, B, stages):
    T = 2 * B
    D = 256
    C = D // P
    top = ExitStack()
    with top:
        def sb(ctx, name, shape, dt=F32):
            return ctx.enter_context(nc.sbuf_tensor(name, shape, dt))

        def sem(ctx, name):
            made = ctx.enter_context(nc.semaphore(name))
            ctx.used.append(made.num)
            return made

        x_all = sb(top, "x_all", [P, T + 2, D])
        ident = sb(top, "ident", [P, P])
        own_rows = sb(top, "own_rows", [P, 4])
        half_rows = sb(top, "half_rows", [P, 2])
        gates = sb(top, "gates", [P, 8])
        st = sb(top, "st", [P, 2, 6])
        mv = sb(top, "mv", [P, 2, 2])
        base = sb(top, "base", [P, 32])
        rstd = sb(top, "rstd", [P, 32])
        minus_half = sb(top, "minus_half", [P, 32])
        ring = top.enter_context(nc.psum_tensor("ring", [P, RING, 1024], F32))
        acc = top.enter_context(nc.psum_tensor("acc", [P, ACCS, 512], F32))

        def rotations(ctx, tag, ring_order, acc_order):
            full = [sem(ctx, f"{tag}_ring_full{i}") for i in range(RING)]
            taken = [sem(ctx, f"{tag}_ring_taken{i}") for i in range(RING)]
            afull = [sem(ctx, f"{tag}_acc_full{i}") for i in range(ACCS)]
            ataken = [sem(ctx, f"{tag}_acc_taken{i}") for i in range(ACCS)]
            return Rotation(ring_order, RING, full, taken), Rotation(acc_order, ACCS, afull, ataken)

        def start_over(used):
            numbers = range(min(used), max(used) + 1)
            nc.gpsimd.dma_reset(numbers)
            nc.gpsimd.sem_clear(numbers)
            nc.all_engine_barrier()

        def open_block(ctx):
            if ctx.used:
                ctx.callback(start_over, ctx.used)
            return ctx.enter_context(nc.Block())

        def every(name):
            return a[name].partition_broadcast(P)

        with Stage() as ctx:
            loaded = sem(ctx, "start_loaded")
            made = sem(ctx, "start_made")
            gated = sem(ctx, "start_gated")
            block = open_block(ctx)

            @block.sync
            def _(sp):
                sp.dma_start(x_all[:, 0:T, :], a["x"].rearrange("b (t p) d -> p (b t) d", p=P)).then_inc(loaded, 16)
                sp.dma_start(gates[:, 0:4], every("g_xattn")).then_inc(loaded, 16)
                sp.dma_start(gates[:, 4:8], every("g_ffn")).then_inc(loaded, 16)
                sp.wait_ge(loaded, 48)

            @block.gpsimd
            def _(pool):
                pool.memset(ident[:], 0.0).then_inc(made, 1)
                pool.wait_ge(made, 1)
                pool.affine_select(out=ident[:], in_=ident[:], compare_op=ALU.not_equal, fill=1.0, base=0,
                                   pattern=[[-1, P]], channel_multiplier=1).then_inc(made, 1)
                pool.memset(minus_half[:], -0.5).then_inc(made, 1)
                pool.wait_ge(made, 3)
                pool.memset(own_rows[:], 0.0).then_inc(made, 1)
                pool.memset(half_rows[:], 0.0).then_inc(made, 1)
                pool.wait_ge(made, 5)
                for r in range(4):
                    pool.memset(own_rows[32 * r:32 * r + 32, r:r + 1], 1.0).then_inc(made, 1)
                    pool.wait_ge(made, 6 + r)
                for r in range(2):
                    pool.memset(half_rows[64 * r:64 * r + 64, r:r + 1], 1.0).then_inc(made, 1)
                    pool.wait_ge(made, 10 + r)
                pool.memset(x_all[:, T:T + 2, :], 0.0).then_inc(made, 1)

            @block.scalar
            def _(act):
                act.wait_ge(loaded, 48)
                act.activation(gates[:], gates[:], ACT.Tanh).then_inc(gated, 1)

        def roots(pool, widths, asked, given):
            for i, w in enumerate(widths):
                pool.wait_ge(asked, i + 1)
                pool.tensor_tensor(rstd[:, 0:w], base[:, 0:w], minus_half[:, 0:w], ALU.pow).then_inc(given, 1)

        def ask(link, ins):
            link.asked += 1
            ins.then_inc(link.root_asked, 1)

        def power(dve, link, ins):
            ask(link, ins)
            dve.wait_ge(link.root_given, link.asked)

        def norm_tiles(dve, link, src, dst):
            for t in range(2):
                ins = dve.bn_stats(st[:, t, :], src(t))
            link(ins)
            for t in range(2):
                ins = dve.bn_aggr(mv[:, t, :], st[:, t, :])
            link(ins)
            power(dve, link, dve.tensor_scalar(base[:, 0:2], mv[:, 0:2, 1], EPS, None, ALU.add))
            for t in range(2):
                ins = dve.tensor_scalar(dst(t), src(t), mv[:, t, 0:1], rstd[:, t:t + 1], ALU.subtract, ALU.mult)
            link(ins)

        def norm_batch(dve, link, first_tile, dst, times):
            link(dve.tensor_copy(dst, x_all[:, bass.ds(first_tile, 2), :]))
            for _ in range(times):
                norm_tiles(dve, link, lambda t: dst[:, t, :], lambda t: dst[:, t, :])

        def norm_first_batch(tag, dst, times):
            with Stage() as ctx:
                linked = sem(ctx, f"{tag}_first_linked")
                root_asked = sem(ctx, f"{tag}_first_root_asked")
                root_given = sem(ctx, f"{tag}_first_root_given")
                block = open_block(ctx)

                @block.gpsimd
                def _(pool):
                    roots(pool, [2] * times, root_asked, root_given)

                @block.vector
                def _(dve):
                    norm_batch(dve, chain(dve, linked, root_asked, root_given), 0, dst, times)

        def narrow_pe(pe, rg, ac, tag, w, queries_ready, values_ready):
            q_pad, q_t, k_t, v_pad, probs = w["q_pad"], w["q_t"], w["k_t"], w["v_pad"], w["probs"]

            def queries(name, groups):
                rg.wait_room(pe, name)
                s = rg.slot(name)
                for g in groups:
                    for t in range(2):
                        ins = pe.transpose(ring[:, s, g * 256 + t * P:g * 256 + (t + 1) * P],
                                           q_pad[:, t, 4 * g:4 * g + 4, :].rearrange("p h s -> p (h s)"), ident[:])
                ins.then_inc(rg.full(name), 1)

            def by_query(i):
                name = (tag, "S", i)
                rg.wait_room(pe, name)
                for j in range(2):
                    h = 2 * i + j
                    g, r = h // 4, h % 4
                    for t in range(2):
                        ins = pe.matmul(ring[:, rg.slot(name), 512 * j + 256 * t:512 * j + 256 * t + 256],
                                        q_t[:, r, g, t * P:(t + 1) * P], k_t[:, g, :],
                                        start=True, stop=True, skip_group_check=True)
                ins.then_inc(rg.full(name), 1)

            def by_key(i):
                name = (tag, "T", i)
                rg.wait_room(pe, name)
                for j in range(2):
                    h = 2 * i + j
                    g, r = h // 4, h % 4
                    for k in range(2):
                        o = ring[:, rg.slot(name), 512 * j + 256 * k:512 * j + 256 * k + 256]
                        ins = pe.matmul(o, k_t[:, g, k * P:(k + 1) * P], q_t[:, r, g, :],
                                        start=True, stop="neg_mask_t" not in w, skip_group_check=True)
                        if "neg_mask_t" in w:
                            ins = pe.matmul(o, w["ident_bf"][:], w["neg_mask_t"][:, k, :], start=False, stop=True,
                                            skip_group_check=True)
                ins.then_inc(rg.full(name), 1)

            def values(i):
                rg.wait_taken(pe, (tag, "T", i))
                if i == 0:
                    for t in range(2):
                        ac.wait_room(pe, (tag, "av", t))
                for j in range(2):
                    h = 2 * i + j
                    for t in range(2):
                        for k in range(2):
                            ins = pe.matmul(acc[:, ac.slot((tag, "av", t)), 17 * h:17 * h + 17],
                                            probs[:, i % 3, j, k, t * P:(t + 1) * P], v_pad[:, k, h, 0:17],
                                            start=(k == 0), stop=(k == 1), skip_group_check=True)
                        if h == HEADS - 1:
                            ins.then_inc(ac.full((tag, "av", t)), 1)
                        elif j == 1 and t == 1:
                            ins.then_inc(w["weights_used"], 1)

            queries_ready()
            queries((tag, "Q", 0), range(2))
            queries((tag, "Q", 1), range(2, 4))
            rg.wait_taken(pe, (tag, "Q", 0))
            for i in range(6):
                if i == 4:
                    rg.wait_taken(pe, (tag, "Q", 1))
                by_query(i)
            for i in range(4):
                rg.wait_taken(pe, (tag, "S", i))
            queries((tag, "Q2", 0), range(2))
            by_query(6)
            by_query(7)
            rg.wait_taken(pe, (tag, "Q2", 0))
            by_key(0)
            by_key(1)
            for i in range(4, 8):
                rg.wait_taken(pe, (tag, "S", i))
            queries((tag, "Q2", 1), range(2, 4))
            values_ready()
            for i in range(2, 8):
                if i == 4:
                    rg.wait_taken(pe, (tag, "Q2", 1))
                by_key(i)
                values(i - 2)
            values(6)
            values(7)

        def narrow_act(act, rg, tag, w, scale):
            q_t, probs = w["q_t"], w["probs"]

            def queries(name, g0, g1):
                rg.wait_full(act, name)
                for r in range(4):
                    ins = act.activation(q_t[:, r, g0:g1, :].rearrange("p g n -> p (g n)"), ring[:, rg.slot(name), g0 * 256:g1 * 256],
                                         ACT.Identity, scale=own_rows[:, r:r + 1])
                ins.then_inc(rg.taken(name), 1)

            def weights(i):
                name = (tag, "T", i)
                rg.wait_full(act, name)
                if i >= 3:
                    act.wait_ge(w["weights_used"], w["weights_base"] + i - 2)
                act.activation(probs[:, i % 3, :, :, :].rearrange("p j k n -> p (j k n)"), ring[:, rg.slot(name), :],
                               ACT.Exp, scale=scale).then_inc(rg.taken(name), 1)

            queries((tag, "Q", 0), 0, 2)
            queries((tag, "Q", 1), 2, 4)
            rg.wait_full(act, (tag, "S", 3))
            queries((tag, "Q2", 0), 0, 2)
            weights(0)
            weights(1)
            rg.wait_full(act, (tag, "S", 7))
            queries((tag, "Q2", 1), 2, 4)
            for i in range(2, 8):
                weights(i)

        def narrow_maxima(dve, rg, tag, w):
            for i in range(8):
                name = (tag, "S", i)
                rg.wait_full(dve, name)
                s = ring[:, rg.slot(name), :].rearrange("p (j t n) -> p j t n", j=2, t=2)
                if "neg_mask" not in w:
                    dve.tensor_reduce(w["q_pad"][:, :, 2 * i:2 * i + 2, HD].rearrange("p t h -> p h t"), s, AX.X,
                                      ALU.max, negate=True).then_inc(rg.taken(name), 1)
                    continue
                if i >= 2:
                    rg.wait_taken(dve, (tag, "S", i - 2))
                for j in range(2):
                    for t in range(2):
                        ins = dve.tensor_tensor_reduce(w["junk"][:, 4 * (i % 2) + 2 * j + t, :], s[:, j, t, :],
                                                       w["neg_mask"][:, t, :], -1.0, 3.0e38, ALU.add, ALU.min,
                                                       w["q_pad"][:, t, 2 * i + j, HD:HD + 1])
                ins.then_inc(rg.taken(name), 1)

        def narrow_heads(dve, link, ac, tag, w):
            for t in range(2):
                ac.wait_full(dve, (tag, "av", t))
                o = acc[:, ac.slot((tag, "av", t)), 0:17 * HEADS].rearrange("p (h n) -> p h n", n=17)
                link(dve.reciprocal(w["inv"][:, t, :], o[:, :, HD]))
                ins = dve.tensor_tensor(w["heads"][:, t, :].rearrange("p (h n) -> p h n", n=HD), o[:, :, 0:HD],
                                        w["inv"][:, t, :].unsqueeze(2).to_broadcast([P, HEADS, HD]), ALU.mult)
                ins.then_inc(ac.taken((tag, "av", t)), 1)

        def transpose_tiles(pe, rg, name, src):
            rg.wait_room(pe, name)
            for t in range(2):
                for c in range(C):
                    ins = pe.transpose(ring[:, rg.slot(name), c * 256 + t * P:c * 256 + (t + 1) * P],
                                       src[:, t, c * P:(c + 1) * P], ident[:])
            ins.then_inc(rg.full(name), 1)

        def project(pe, ac, tag, src, w, n=256):
            for t in range(2):
                ac.wait_room(pe, (tag, t))
                for c in range(C):
                    ins = pe.matmul(acc[:, ac.slot((tag, t)), 0:n], src[:, c, t * P:(t + 1) * P], w[:, c, 0:n],
                                    start=(c == 0), stop=(c == C - 1))
                ins.then_inc(ac.full((tag, t)), 1)

        def add_projection(dve, link, ac, tag, xb, gate, bias):
            for t in range(2):
                ac.wait_full(dve, (tag, t))
                dve.scalar_tensor_tensor(out=xb[:, t, :], in0=acc[:, ac.slot((tag, t)), 0:D], scalar=gate, in1=xb[:, t, :],
                                         op0=ALU.mult, op1=ALU.add).then_inc(ac.taken((tag, t)), 1)
            for t in range(2):
                ac.wait_taken(dve, (tag, t))
                ins = dve.tensor_tensor(xb[:, t, :], xb[:, t, :], bias, ALU.add)
            link(ins)

        if "A" in stages:
            with ExitStack() as ph:
                xb = sb(ph, "a_xb", [P, 2, D])
                cb = sb(ph, "a_cb", [P, 2, D])
                wq = sb(ph, "a_wq", [P, C, 1024])
                wkv = sb(ph, "a_wkv", [P, C, 2048])
                wout = sb(ph, "a_wout", [P, 8, D])
                ln_cols = sb(ph, "a_ln_cols", [P, 4, C])
                ln_o = sb(ph, "a_ln_o", [P, 2, D])
                mask_u8 = sb(ph, "a_mask_u8", [P, B, 256], U8)
                neg_keys = sb(ph, "a_neg_keys", [P, 512])
                fq = sb(ph, "a_fq", [P, C, D])
                fk = sb(ph, "a_fk", [P, C, 4 * P])
                fv = sb(ph, "a_fv", [P, C, D])
                fp = sb(ph, "a_fp", [P, C, D])
                frs = sb(ph, "a_frs", [P, C, 17])
                fk_bias = sb(ph, "a_fk_bias", [P, 4])
                rows = sb(ph, "a_rows", [P, 5, D])
                rs_bias = sb(ph, "a_rs_bias", [P, 17])
                temp = sb(ph, "a_temp", [P, 5, HEADS])
                w1 = sb(ph, "a_w1", [P, C, D])
                normed = sb(ph, "a_normed", [P, 4, D])
                kv_t = sb(ph, "a_kv_t", [P, C, 512])
                q16 = sb(ph, "a_q16", [P, HEADS, D])
                k8 = sb(ph, "a_k8", [P, 8, 512])
                v4 = sb(ph, "a_v4", [P, 4, 1024])
                masked = sb(ph, "a_masked", [P, 2, 2, 512])
                wide_p = sb(ph, "a_wide_p", [P, 4, 2, 512])
                wide_pt = sb(ph, "a_wide_pt", [P, 2, 1024])
                row_min = sb(ph, "a_row_min", [P, HEADS, 2])
                row_sum = sb(ph, "a_row_sum", [P, 2, HEADS])
                inv = sb(ph, "a_inv", [P, 2, HEADS])
                heads = sb(ph, "a_heads", [P, 2, 1024])
                q_pad = sb(ph, "a_q_pad", [P, 2, HEADS, SLOT])
                v_pad = sb(ph, "a_v_pad", [P, 2, HEADS, SLOT])
                small = sb(ph, "a_small", [P, 2, 64])
                heads_t = q16
                x_t = kv_t
                q_t = k8[:].rearrange("p a n -> p (a n)").rearrange("p (r g n) -> p r g n", r=4, g=4)
                k_t = masked[:, 0, :, :].rearrange("p a n -> p (a n)").rearrange("p (g n) -> p g n", g=4)
                narrow_heads_sb = heads[:, :, 0:D]
                work = heads[:, :, 256:768]
                probs = v4[:, 0:3, :].rearrange("p i (j k n) -> p i j k n", j=2, k=2)

                with Stage() as ctx:
                    loaded = sem(ctx, "a_loaded")
                    made = sem(ctx, "a_made")
                    linked = sem(ctx, "a_linked")
                    stepped = sem(ctx, "a_stepped")
                    block = open_block(ctx)
                    loads = [
                        (wq[:], a["L0_xattn_Wq"].rearrange("(c p) n -> p c n", p=P)),
                        (wkv[:], a["L0_xattn_Wkv"].rearrange("(c p) n -> p c n", p=P)),
                        (wout[:], a["L0_xattn_Wout"].rearrange("(c p) n -> p c n", p=P)),
                        (ln_cols[:, 0, :], a["ln_x_g_cols"]), (ln_cols[:, 1, :], a["ln_x_b_cols"]),
                        (ln_cols[:, 2, :], a["ln_l_g_cols"]), (ln_cols[:, 3, :], a["ln_l_b_cols"]),
                        (ln_o[:, 0, :], every("L0_xattn_ln_o_g")), (ln_o[:, 1, :], every("L0_xattn_ln_o_b")),
                        (mask_u8[:], every("mask_keys")),
                        (fq[:], a["fq_t"].rearrange("(c p) n -> p c n", p=P)),
                        (fk[:], a["fk_t"].rearrange("(c p) n -> p c n", p=P)),
                        (fv[:], a["fv_t"].rearrange("(c p) n -> p c n", p=P)),
                        (fp[:], a["fp_t"].rearrange("(c p) n -> p c n", p=P)),
                        (frs[:], a["frs_t"].rearrange("(c p) n -> p c n", p=P)),
                        (fk_bias[:], a["fk_bias"]),
                        (rows[:, 0, :], every("L0_ffn_bq")), (rows[:, 1, :], every("L0_ffn_bv")),
                        (rows[:, 2, :], every("L0_ffn_bp")), (rows[:, 3, :], every("query_row")),
                        (rows[:, 4, :], every("L1_xattn_b_out")),
                        (rs_bias[:, 0:15], every("L0_ffn_br")), (rs_bias[:, 15:17], every("L0_ffn_bs")),
                        (temp[:, 0, :], every("temperature_row")),
                        (w1[:], a["w1_t"].rearrange("(c p) n -> p c n", p=P)),
                    ]

                    @block.sync
                    def _(sp):
                        for dst, src in loads:
                            sp.dma_start(dst, src).then_inc(loaded, 16)
                        sp.wait_ge(loaded, 16 * len(loads))

                    @block.gpsimd
                    def _(pool):
                        pool.memset(q_pad[:], 0.0).then_inc(made, 1)
                        pool.memset(v_pad[:], 1.0).then_inc(made, 1)
                        pool.memset(neg_keys[:], 0.0).then_inc(made, 1)
                        pool.wait_ge(made, 3)

                    @block.scalar
                    def _(act):
                        act.wait_ge(stepped, 1)
                        act.activation(temp[:, 2, :], temp[:, 1, :], ACT.Exp).then_inc(stepped, 1)
                        act.wait_ge(stepped, 3)
                        act.activation(temp[:, 4, :], temp[:, 3, :], ACT.Ln).then_inc(stepped, 1)

                    @block.vector
                    def _(dve):
                        link = chain(dve, linked)
                        dve.wait_ge(loaded, 16 * len(loads))
                        link(dve.tensor_scalar(small[:, 0, 0:16], temp[:, 0, :], 0.0, None, ALU.max))
                        dve.scalar_tensor_tensor(out=temp[:, 1, :], in0=small[:, 0, 0:16], scalar=-2.0, in1=temp[:, 0, :],
                                                 op0=ALU.mult, op1=ALU.add).then_inc(stepped, 1)
                        dve.wait_ge(stepped, 2)
                        dve.tensor_scalar(temp[:, 3, :], temp[:, 2, :], 1.0, None, ALU.add).then_inc(stepped, 1)
                        for i in range(2):
                            dve.tensor_scalar(ln_o[:, i, :], ln_o[:, i, :], gates[:, 0:1], None, ALU.mult)
                        dve.tensor_scalar(rows[:, 2, :], rows[:, 2, :], gates[:, 4:5], None, ALU.mult)
                        dve.tensor_scalar(rows[:, 4, :], rows[:, 4, :], gates[:, 1:2], None, ALU.mult)
                        dve.wait_ge(stepped, 4)
                        link(dve.tensor_tensor(temp[:, 0, :], temp[:, 4, :], small[:, 0, 0:16], ALU.add))
                        link(dve.tensor_scalar(temp[:, 0, :], temp[:, 0, :], HD ** -0.5, None, ALU.mult))

                ring_order = [("xT",), ("q", 0), ("lT",), ("q", 1)] + [("k", i) for i in range(4)] + [("v", i) for i in range(4)]
                for i in range(HEADS + PT_LAG):
                    ring_order += [("S", i)] * (i < HEADS) + [("PT", i - PT_LAG)] * (i >= PT_LAG)
                ring_order += [("OT", 0), ("OT", 1), ("fxT",), ("fq",), ("fv",), ("fk",)] + narrow_order("f") + [("fHT",)]
                ring_order += [("cT",)] + narrow_order("c") + [("cHT",)]
                acc_order = [("av", half, t) for half in range(2) for t in range(2)] + [("wo", t) for t in range(2)]
                acc_order += [("f", "av", t) for t in range(2)] + [("gate", t) for t in range(2)] + [("fp", t) for t in range(2)]
                acc_order += [("c", "av", t) for t in range(2)] + [("cp", t) for t in range(2)]

                norm_first_batch("a", normed[:, 2:4, :], 2)
                with nc.Fori(0, B) as b, Stage() as ctx:
                    rg, ac = rotations(ctx, "a", ring_order, acc_order)
                    linked = sem(ctx, "a_dve_linked")
                    root_asked = sem(ctx, "a_root_asked")
                    root_given = sem(ctx, "a_root_given")
                    context_loaded = sem(ctx, "a_context_loaded")
                    masked_ready = sem(ctx, "a_masked_ready")
                    weights_ready = sem(ctx, "a_weights_ready")
                    normed_ready = sem(ctx, "a_normed_ready")
                    heads_ready = sem(ctx, "a_heads_ready")
                    queries_ready = sem(ctx, "a_queries_ready")
                    weights_used = sem(ctx, "a_weights_used")
                    gate_logits = sem(ctx, "a_gate_logits")
                    gate_exps = sem(ctx, "a_gate_exps")
                    block = open_block(ctx)
                    common = dict(q_pad=q_pad, q_t=q_t, k_t=k_t, v_pad=v_pad, probs=probs, inv=inv,
                                  heads=narrow_heads_sb, weights_used=weights_used)
                    wf = dict(common, weights_base=0)
                    wc = dict(common, weights_base=7)

                    @block.tensor
                    def _(pe):
                        def features(name, tile):
                            rg.wait_room(pe, name)
                            for t in range(2):
                                for c in range(C):
                                    ins = pe.transpose(ring[:, rg.slot(name), c * 256 + t * P:c * 256 + (t + 1) * P],
                                                       normed[:, tile + t, c * P:(c + 1) * P], ident[:])
                            ins.then_inc(rg.full(name), 1)

                        def wide_queries(i):
                            rg.wait_room(pe, ("q", i))
                            for j in range(4):
                                for c in range(C):
                                    ins = pe.matmul(ring[:, rg.slot(("q", i)), 256 * j:256 * j + 256],
                                                    wq[:, c, (4 * i + j) * P:(4 * i + j + 1) * P], kv_t[:, c, 256:512],
                                                    start=(c == 0), stop=(c == C - 1), skip_group_check=True)
                            ins.then_inc(rg.full(("q", i)), 1)

                        features(("xT",), 2)
                        rg.wait_taken(pe, ("xT",))
                        wide_queries(0)
                        pe.wait_ge(normed_ready, 1)
                        features(("lT",), 0)
                        wide_queries(1)
                        rg.wait_taken(pe, ("lT",))
                        for i in range(4):
                            rg.wait_room(pe, ("k", i))
                            for j in range(2):
                                for c in range(C):
                                    ins = pe.matmul(ring[:, rg.slot(("k", i)), 512 * j:512 * j + 512],
                                                    wkv[:, c, (2 * i + j) * P:(2 * i + j + 1) * P], kv_t[:, c, :],
                                                    start=(c == 0), stop=(c == C - 1))
                            ins.then_inc(rg.full(("k", i)), 1)
                        for i in range(4):
                            rg.wait_room(pe, ("v", i))
                            for j in range(2):
                                for c in range(C):
                                    ins = pe.matmul(ring[:, rg.slot(("v", i)), 512 * j:512 * j + 512],
                                                    kv_t[:, c, i * P:(i + 1) * P], wkv[:, c, 1024 + 512 * j:1536 + 512 * j],
                                                    start=(c == 0), stop=(c == C - 1))
                            ins.then_inc(rg.full(("v", i)), 1)
                        for i in range(2):
                            rg.wait_taken(pe, ("q", i))
                        for i in range(4):
                            rg.wait_taken(pe, ("k", i))

                        def scores(h):
                            rg.wait_room(pe, ("S", h))
                            for t in range(2):
                                ins = pe.matmul(ring[:, rg.slot(("S", h)), 512 * t:512 * t + 512],
                                                q16[:, h, t * P:(t + 1) * P], k8[:, h // 2, :], start=True, stop=True)
                            ins.then_inc(rg.full(("S", h)), 1)

                        def weights_by_key(h):
                            pe.wait_ge(weights_ready, h + 1)
                            rg.wait_room(pe, ("PT", h))
                            for k in range(4):
                                for t in range(2):
                                    ins = pe.transpose(ring[:, rg.slot(("PT", h)), 256 * k + P * t:256 * k + P * t + P],
                                                       wide_p[:, h % 4, t, k * P:(k + 1) * P], ident[:])
                            ins.then_inc(rg.full(("PT", h)), 1)

                        def head_values(h):
                            half = h // 8
                            rg.wait_taken(pe, ("PT", h))
                            if h == 0:
                                for i in range(4):
                                    rg.wait_taken(pe, ("v", i))
                            for t in range(2):
                                name = ("av", half, t)
                                if h % 8 == 0:
                                    ac.wait_room(pe, name)
                                for k in range(4):
                                    ins = pe.matmul(acc[:, ac.slot(name), 64 * (h % 8):64 * (h % 8) + 64],
                                                    wide_pt[:, h % 2, 256 * k + P * t:256 * k + P * t + P],
                                                    v4[:, k, 64 * h:64 * h + 64], start=(k == 0), stop=(k == 3),
                                                    skip_group_check=True)
                                if h % 8 == 7:
                                    ins.then_inc(ac.full(name), 1)

                        for i in range(HEADS + AV_LAG):
                            if i < HEADS:
                                scores(i)
                            if PT_LAG <= i < HEADS + PT_LAG:
                                weights_by_key(i - PT_LAG)
                            if i >= AV_LAG:
                                head_values(i - AV_LAG)
                        pe.wait_ge(heads_ready, 1)
                        for i in range(2):
                            rg.wait_room(pe, ("OT", i))
                            for j in range(4):
                                for t in range(2):
                                    ins = pe.transpose(ring[:, rg.slot(("OT", i)), 256 * j + P * t:256 * j + P * t + P],
                                                       heads[:, t, (4 * i + j) * P:(4 * i + j + 1) * P], ident[:])
                            ins.then_inc(rg.full(("OT", i)), 1)
                        for i in range(2):
                            rg.wait_taken(pe, ("OT", i))
                        for t in range(2):
                            ac.wait_room(pe, ("wo", t))
                            for j in range(8):
                                ins = pe.matmul(acc[:, ac.slot(("wo", t)), 0:D], heads_t[:, j, t * P:(t + 1) * P], wout[:, j, :],
                                                start=(j == 0), stop=(j == 7))
                            ins.then_inc(ac.full(("wo", t)), 1)

                        pe.wait_ge(normed_ready, 2)
                        transpose_tiles(pe, rg, ("fxT",), normed)
                        rg.wait_taken(pe, ("fxT",))
                        for name, w in ((("fq",), fq), (("fv",), fv)):
                            rg.wait_room(pe, name)
                            for t in range(2):
                                for c in range(C):
                                    ins = pe.matmul(ring[:, rg.slot(name), 256 * t:256 * t + 256],
                                                    x_t[:, c, t * P:(t + 1) * P], w[:, c, :], start=(c == 0), stop=(c == C - 1),
                                                    skip_group_check=True)
                            ins.then_inc(rg.full(name), 1)
                        rg.wait_room(pe, ("fk",))
                        for g in range(4):
                            for c in range(C):
                                ins = pe.matmul(ring[:, rg.slot(("fk",)), 256 * g:256 * g + 256], fk[:, c, g * P:(g + 1) * P],
                                                x_t[:, c, 0:256], start=(c == 0), stop=(c == C - 1), skip_group_check=True)
                        ins.then_inc(rg.full(("fk",)), 1)
                        rg.wait_taken(pe, ("fk",))
                        narrow_pe(pe, rg, ac, "f", wf, lambda: pe.wait_ge(queries_ready, 1),
                                  lambda: rg.wait_taken(pe, ("fv",)))
                        for t in range(2):
                            ac.wait_taken(pe, ("f", "av", t))
                        transpose_tiles(pe, rg, ("fHT",), narrow_heads_sb)
                        rg.wait_taken(pe, ("fHT",))
                        project(pe, ac, "gate", heads_t, frs, 17)
                        project(pe, ac, "fp", heads_t, fp)

                        pe.wait_ge(queries_ready, 2)
                        rg.wait_room(pe, ("cT",))
                        for g in range(4):
                            for t in range(2):
                                ins = pe.transpose(ring[:, rg.slot(("cT",)), 256 * g + P * t:256 * g + P * t + P],
                                                   v_pad[:, t, 4 * g:4 * g + 4, :].rearrange("p h s -> p (h s)"), ident[:])
                        ins.then_inc(rg.full(("cT",)), 1)
                        rg.wait_taken(pe, ("cT",))
                        narrow_pe(pe, rg, ac, "c", wc, lambda: pe.wait_ge(queries_ready, 3), lambda: None)
                        for t in range(2):
                            ac.wait_taken(pe, ("c", "av", t))
                        transpose_tiles(pe, rg, ("cHT",), narrow_heads_sb)
                        rg.wait_taken(pe, ("cHT",))
                        project(pe, ac, "cp", heads_t, w1)

                    @block.scalar
                    def _(act):
                        def features(name, column, i):
                            rg.wait_full(act, name)
                            for c in range(C):
                                ins = act.activation(kv_t[:, c, column:column + 256], ring[:, rg.slot(name), 256 * c:256 * c + 256],
                                                     ACT.Identity, scale=ln_cols[:, 2 * i, c:c + 1], bias=ln_cols[:, 2 * i + 1, c:c + 1])
                            ins.then_inc(rg.taken(name), 1)

                        def wide_queries(i):
                            rg.wait_full(act, ("q", i))
                            for r in range(2):
                                ins = act.activation(q16[:, 8 * i + r:8 * i + 8:2, :], ring[:, rg.slot(("q", i)), :].rearrange("p (j n) -> p j n", j=4),
                                                     ACT.Identity, scale=half_rows[:, r:r + 1])
                            ins.then_inc(rg.taken(("q", i)), 1)

                        features(("xT",), 256, 1)
                        wide_queries(0)
                        features(("lT",), 0, 0)
                        wide_queries(1)
                        for i in range(4):
                            rg.wait_full(act, ("k", i))
                            act.activation(k8[:, 2 * i:2 * i + 2, :].rearrange("p j n -> p (j n)"), ring[:, rg.slot(("k", i)), :],
                                           ACT.Copy).then_inc(rg.taken(("k", i)), 1)
                        for h in range(HEADS):
                            act.wait_ge(masked_ready, h + 1)
                            if h >= 4:
                                rg.wait_full(act, ("PT", h - 4))
                            for t in range(2):
                                ins = act.activation(wide_p[:, h % 4, t, :], masked[:, h % 2, t, :], ACT.Exp, scale=-1.0,
                                                     bias=row_min[:, h, t:t + 1], accum_out=row_sum[:, t, h:h + 1])
                            ins.then_inc(weights_ready, 1)
                        for i in range(2):
                            rg.wait_full(act, ("OT", i))
                            act.activation(heads_t[:, 4 * i:4 * i + 4, :].rearrange("p j n -> p (j n)"), ring[:, rg.slot(("OT", i)), :],
                                           ACT.Copy).then_inc(rg.taken(("OT", i)), 1)

                        def copy_tiles(name, dst):
                            rg.wait_full(act, name)
                            act.activation(dst[:, 0:2, 0:256], ring[:, rg.slot(name), 0:512].rearrange("p (c n) -> p c n", c=2),
                                           ACT.Copy).then_inc(rg.taken(name), 1)

                        copy_tiles(("fxT",), x_t)
                        narrow_act(act, rg, "f", wf, 1.0)
                        copy_tiles(("fHT",), heads_t)
                        act.wait_ge(gate_logits, 1)
                        for t in range(2):
                            act.activation(small[:, t, 32:47], small[:, t, 0:15], ACT.Exp, bias=small[:, t, 28:29],
                                           accum_out=small[:, t, 48:49])
                            act.activation(small[:, t, 50:53], small[:, t, 17:20], ACT.Exp, bias=small[:, t, 28:29],
                                           accum_out=small[:, t, 53:54])
                            ins = act.activation(small[:, t, 54:56], small[:, t, 15:17], ACT.Exp, bias=small[:, t, 29:30],
                                                 accum_out=small[:, t, 56:57])
                        ins.then_inc(gate_exps, 1)
                        rg.wait_full(act, ("cT",))
                        act.activation(k_t.rearrange("p g n -> p (g n)"), ring[:, rg.slot(("cT",)), :], ACT.Copy).then_inc(rg.taken(("cT",)), 1)
                        narrow_act(act, rg, "c", wc, HD ** -0.5)
                        copy_tiles(("cHT",), heads_t)

                    @block.sync
                    def _(sp):
                        sp.dma_start(cb[:], a["ctx_1024"].rearrange("b (t p) d -> b p t d", p=P)[bass.ds(b, 1)].rearrange("o p t d -> (o p) t d"))\
                          .then_inc(context_loaded, 16)

                    @block.gpsimd
                    def _(pool):
                        roots(pool, [2, 2, 2, 32, 2, 2, 2], root_asked, root_given)

                    @block.vector
                    def _(dve):
                        link = chain(dve, linked, root_asked, root_given)
                        dve.tensor_copy(xb[:], x_all[:, bass.ds(b * 2, 2), :])
                        link(dve.tensor_scalar(neg_keys[:, 0:256], mask_u8[:, bass.ds(b, 1), :].rearrange("p o n -> p (o n)"),
                                               FLT_MAX, -FLT_MAX, ALU.mult, ALU.add))
                        dve.wait_ge(context_loaded, 16)
                        norm_tiles(dve, link, lambda t: cb[:, t, :], lambda t: normed[:, t, :])
                        dve.engine_nop().then_inc(normed_ready, 1)
                        for i in range(4):
                            rg.wait_full(dve, ("v", i))
                            dve.tensor_copy(v4[:, i, :], ring[:, rg.slot(("v", i)), :]).then_inc(rg.taken(("v", i)), 1)

                        def mask_scores(h):
                            rg.wait_full(dve, ("S", h))
                            if h >= 2:
                                dve.wait_ge(weights_ready, h - 1)
                            for t in range(2):
                                ins = dve.tensor_tensor_reduce(masked[:, h % 2, t, :], ring[:, rg.slot(("S", h)), 512 * t:512 * t + 512],
                                                               neg_keys[:], -0.125, 3.0e38, ALU.add, ALU.min, row_min[:, h, t:t + 1])
                            ins.then_inc(masked_ready, 1)
                            dve.wait_ge(masked_ready, h + 1)
                            dve.engine_nop().then_inc(rg.taken(("S", h)), 1)

                        def take_weights(h):
                            rg.wait_full(dve, ("PT", h))
                            if h >= 8:
                                ac.wait_full(dve, ("av", 0, 1))
                            dve.tensor_copy(wide_pt[:, h % 2, :], ring[:, rg.slot(("PT", h)), :]).then_inc(rg.taken(("PT", h)), 1)

                        def wide_heads(half):
                            for t in range(2):
                                name = ("av", half, t)
                                ac.wait_full(dve, name)
                                if t == 0:
                                    dve.wait_ge(weights_ready, 8 * half + 8)
                                    link(dve.reciprocal(inv[:, :, 8 * half:8 * half + 8], row_sum[:, :, 8 * half:8 * half + 8]))
                                dve.tensor_tensor(heads[:, t, 512 * half:512 * half + 512].rearrange("p (h n) -> p h n", n=64),
                                                  acc[:, ac.slot(name), :].rearrange("p (h n) -> p h n", n=64),
                                                  inv[:, t, 8 * half:8 * half + 8].unsqueeze(2).to_broadcast([P, 8, 64]),
                                                  ALU.mult).then_inc(ac.taken(name), 1)

                        for i in range(HEADS + PT_LAG):
                            if i < HEADS:
                                mask_scores(i)
                            if i >= PT_LAG:
                                take_weights(i - PT_LAG)
                            if i == 8 + AV_LAG:
                                wide_heads(0)
                        wide_heads(1)
                        for t in range(2):
                            ac.wait_taken(dve, ("av", 1, t))
                        dve.engine_nop().then_inc(heads_ready, 1)
                        for t in range(2):
                            ac.wait_full(dve, ("wo", t))
                        o = lambda t: acc[:, ac.slot(("wo", t)), 0:D]
                        for t in range(2):
                            ins = dve.bn_stats(st[:, t, :], o(t))
                        link(ins)
                        for t in range(2):
                            ins = dve.bn_aggr(mv[:, t, :], st[:, t, :])
                        link(ins)
                        power(dve, link, dve.tensor_scalar(base[:, 0:2], mv[:, 0:2, 1], EPS, None, ALU.add))
                        for t in range(2):
                            dve.scalar_tensor_tensor(out=work[:, t, 0:D], in0=o(t), scalar=mv[:, t, 0:1], in1=ln_o[:, 0, :],
                                                     op0=ALU.subtract, op1=ALU.mult).then_inc(ac.taken(("wo", t)), 1)
                        for t in range(2):
                            ins = dve.tensor_tensor(xb[:, t, :], xb[:, t, :], ln_o[:, 1, :], ALU.add)
                        link(ins)
                        for t in range(2):
                            ins = dve.scalar_tensor_tensor(out=xb[:, t, :], in0=work[:, t, 0:D], scalar=rstd[:, t:t + 1], in1=xb[:, t, :],
                                                           op0=ALU.mult, op1=ALU.add)
                        link(ins)

                        norm_tiles(dve, link, lambda t: xb[:, t, :], lambda t: normed[:, t, :])
                        dve.engine_nop().then_inc(normed_ready, 1)
                        rg.wait_full(dve, ("fq",))
                        qf = work[:, :, 0:256]
                        sq = work[:, :, 256:512]
                        for t in range(2):
                            ins = dve.tensor_tensor(qf[:, t, :], ring[:, rg.slot(("fq",)), 256 * t:256 * t + 256], rows[:, 0, :], ALU.add)
                        ins.then_inc(rg.taken(("fq",)), 1)
                        rg.wait_taken(dve, ("fq",))
                        link(dve.tensor_tensor(sq, qf, qf, ALU.mult))
                        ask(link, dve.tensor_reduce(base[:].rearrange("p (t h) -> p t h", t=2),
                                                    sq.rearrange("p t (h n) -> p t h n", n=HD), AX.X, ALU.add))
                        rg.wait_full(dve, ("fv",))
                        for t in range(2):
                            ins = dve.tensor_tensor(v_pad[:, t, :, 0:HD], ring[:, rg.slot(("fv",)), 256 * t:256 * t + 256].rearrange("p (h n) -> p h n", n=HD),
                                                    rows[:, 1, :].rearrange("p (h n) -> p h n", n=HD), ALU.add)
                        ins.then_inc(rg.taken(("fv",)), 1)
                        rg.wait_full(dve, ("fk",))
                        dve.tensor_tensor(k_t, ring[:, rg.slot(("fk",)), :].rearrange("p (g n) -> p g n", g=4),
                                          fk_bias[:].unsqueeze(2).to_broadcast([P, 4, 256]), ALU.add).then_inc(rg.taken(("fk",)), 1)
                        dve.wait_ge(link.root_given, link.asked)
                        for t in range(2):
                            ins = dve.tensor_tensor(sq[:, t, :].rearrange("p (h n) -> p h n", n=HD), qf[:, t, :].rearrange("p (h n) -> p h n", n=HD),
                                                    rstd[:, 16 * t:16 * t + 16].unsqueeze(2).to_broadcast([P, HEADS, HD]), ALU.mult)
                        link(ins)
                        for t in range(2):
                            ins = dve.tensor_tensor(qf[:, t, :], sq[:, t, :], rows[:, 3, :], ALU.add)
                        link(ins)
                        for t in range(2):
                            ins = dve.tensor_tensor(q_pad[:, t, :, 0:HD], qf[:, t, :].rearrange("p (h n) -> p h n", n=HD),
                                                    temp[:, 0, :].unsqueeze(2).to_broadcast([P, HEADS, HD]), ALU.mult)
                        dve.memset(q_pad[:, :, :, HD:HD + 1], 0.0).then_inc(queries_ready, 1)
                        dve.wait_ge(queries_ready, 1)
                        narrow_maxima(dve, rg, "f", wf)
                        narrow_heads(dve, link, ac, "f", wf)
                        for t in range(2):
                            ac.wait_full(dve, ("gate", t))
                            dve.tensor_tensor(small[:, t, 0:17], acc[:, ac.slot(("gate", t)), 0:17], rs_bias[:], ALU.add).then_inc(ac.taken(("gate", t)), 1)
                        for t in range(2):
                            ac.wait_taken(dve, ("gate", t))
                        for t in range(2):
                            dve.max(small[:, t, 17:25], small[:, t, 0:15])
                        link(dve.tensor_reduce(small[:, :, 29:30], small[:, :, 15:17], AX.X, ALU.max, negate=True))
                        dve.tensor_scalar(small[:, :, 28:29], small[:, :, 17:18], -1.0, None, ALU.mult).then_inc(gate_logits, 1)
                        dve.wait_ge(gate_exps, 1)
                        link(dve.reciprocal(small[:, :, 57:58], small[:, :, 48:49]))
                        link(dve.reciprocal(small[:, :, 58:59], small[:, :, 56:57]))
                        link(dve.tensor_tensor(small[:, :, 59:60], small[:, :, 53:54], small[:, :, 57:58], ALU.mult))
                        link(dve.tensor_tensor(small[:, :, 60:62], small[:, :, 54:56], small[:, :, 58:59].to_broadcast([P, 2, 2]), ALU.mult))
                        link(dve.tensor_scalar(small[:, :, 59:60], small[:, :, 59:60], 3.0, None, ALU.mult))
                        link(dve.tensor_tensor(small[:, :, 62:63], small[:, :, 61:62], small[:, :, 59:60], ALU.mult))
                        link(dve.tensor_tensor(small[:, :, 59:60], small[:, :, 60:61], small[:, :, 61:62], ALU.add))
                        link(dve.tensor_tensor(small[:, :, 63:64], small[:, :, 60:61], small[:, :, 59:60], ALU.mult))
                        link(dve.tensor_tensor(small[:, :, 62:63], small[:, :, 62:63], small[:, :, 63:64], ALU.add))
                        link(dve.tensor_scalar(small[:, :, 62:63], small[:, :, 62:63], 2.0, gates[:, 4:5], ALU.mult, ALU.mult))
                        for t in range(2):
                            ac.wait_full(dve, ("fp", t))
                            dve.scalar_tensor_tensor(out=xb[:, t, :], in0=acc[:, ac.slot(("fp", t)), 0:D], scalar=small[:, t, 62:63],
                                                     in1=xb[:, t, :], op0=ALU.mult, op1=ALU.add).then_inc(ac.taken(("fp", t)), 1)
                        for t in range(2):
                            ac.wait_taken(dve, ("fp", t))
                        for t in range(2):
                            ins = dve.tensor_tensor(xb[:, t, :], xb[:, t, :], rows[:, 2, :], ALU.add)
                        link(ins)

                        for t in range(2):
                            ins = dve.tensor_copy(v_pad[:, t, :, 0:HD], cb[:, t, :].rearrange("p (h n) -> p h n", n=HD))
                        ins.then_inc(queries_ready, 1)
                        dve.memset(q_pad[:, :, :, HD:HD + 1], 0.0)
                        norm_tiles(dve, link, lambda t: xb[:, t, :], lambda t: normed[:, t, :])
                        for t in range(2):
                            ins = dve.tensor_copy(q_pad[:, t, :, 0:HD], normed[:, t, :].rearrange("p (h n) -> p h n", n=HD))
                        ins.then_inc(queries_ready, 1)
                        dve.wait_ge(queries_ready, 3)
                        narrow_maxima(dve, rg, "c", wc)
                        norm_batch(dve, link, b * 2 + 2, normed[:, 2:4, :], 2)
                        narrow_heads(dve, link, ac, "c", wc)
                        add_projection(dve, link, ac, "cp", xb, gates[:, 1:2], rows[:, 4, :])
                        dve.tensor_copy(x_all[:, bass.ds(b * 2, 2), :], xb[:])

        def expert_layer(tag, K, HW, gate, w_route, bias, w_shared, w_experts):
            N = T * P
            E = w_experts.shape[0]
            GT = 4
            G = T // GT
            I = HW // P
            per_turn = 9 if K == 1 else 16
            blocks = E + (K * N - E) // P
            turns = -(-blocks // per_turn)
            NB = turns * per_turn
            TE = T * E
            token_of_slot = nc.dram_tensor(f"{tag}_token_of_slot", (NB * P, 1), F32, kind="Internal").ap()
            x_rows = nc.dram_tensor(f"{tag}_x_rows", (N, D), F32, kind="Internal").ap()
            y_rows = nc.dram_tensor(f"{tag}_y_rows", (NB * P, D), F32, kind="Internal").ap()

            with ExitStack() as ph:
                def s_(name, shape, dt=F32, where=ph):
                    return sb(where, f"{tag}_{name}", shape, dt)

                slots = s_("slots", [P, K, T], U32)
                shares = s_("shares", [P, K, T])
                block_expert = s_("block_expert", [1, NB], I32)
                token_idx = s_("token_idx", [P, NB], U32)
                x4 = s_("x4", [P, GT, D])

                with ExitStack() as pr:
                    xt_all = s_("xt_all", [P, C, N], F32, pr)
                    logits = s_("logits", [P, T, E], F32, pr)
                    wr = s_("wr", [P, C, E], F32, pr)
                    br = s_("br", [P, E], F32, pr)
                    ws = s_("ws", [P, 3072], F32, pr)
                    xn = s_("xn", [P, GT, D], F32, pr)
                    xs = s_("xs", [P, GT, D], F32, pr)
                    top1 = s_("top1", [P, GT], F32, pr)
                    score = s_("score", [P, GT], F32, pr)
                    x_t = s_("x_t", [P, C, 512], F32, pr)

                    with Stage() as ctx:
                        loaded = sem(ctx, f"{tag}_loaded")
                        zeroed = sem(ctx, f"{tag}_zeroed")
                        block = open_block(ctx)

                        @block.vector
                        def _(dve):
                            dve.memset(token_idx[:], 0).then_inc(zeroed, 1)
                            if bias is None:
                                dve.memset(br[:], 0.0)

                        @block.sync
                        def _(sp):
                            sp.dma_start(wr[:], w_route.rearrange("(c p) n -> p c n", p=P)).then_inc(loaded, 16)
                            sp.dma_start(ws[:], w_shared).then_inc(loaded, 16)
                            n = 48
                            if bias is not None:
                                sp.dma_start(br[:], bias.partition_broadcast(P)).then_inc(loaded, 16)
                                n += 16
                            sp.wait_ge(zeroed, 1)
                            sp.dma_start(token_of_slot.rearrange("(p n) o -> p (n o)", p=P), token_idx[:].bitcast(F32)).then_inc(loaded, 16)
                            sp.wait_ge(loaded, n)

                    with nc.Fori(0, G) as g, Stage() as ctx:
                        rg, ac = rotations(ctx, f"{tag}n", [("xt",)], [("lg",)])
                        linked = sem(ctx, f"{tag}n_linked")
                        root_asked = sem(ctx, f"{tag}n_root_asked")
                        root_given = sem(ctx, f"{tag}n_root_given")
                        normed_ready = sem(ctx, f"{tag}n_normed_ready")
                        kept = sem(ctx, f"{tag}n_kept")
                        topped = sem(ctx, f"{tag}n_topped")
                        scored = sem(ctx, f"{tag}n_scored")
                        rows_ready = sem(ctx, f"{tag}n_rows_ready")
                        stored = sem(ctx, f"{tag}n_stored")
                        block = open_block(ctx)

                        @block.gpsimd
                        def _(pool):
                            roots(pool, [2, 2], root_asked, root_given)

                        @block.vector
                        def _(dve):
                            link = chain(dve, linked, root_asked, root_given)
                            link(dve.tensor_copy(x4[:], x_all[:, bass.ds(g * GT, GT), :]))
                            for h in range(2):
                                norm_tiles(dve, link, lambda t: x4[:, 2 * h + t, :], lambda t: xn[:, 2 * h + t, :])
                            dve.engine_nop().then_inc(normed_ready, 1)
                            ac.wait_full(dve, ("lg",))
                            lg = acc[:, 0, 0:GT * E].rearrange("p (t e) -> p t e", t=GT)
                            link(dve.tensor_tensor(logits[:, bass.ds(g * GT, GT), :], lg, br[:].unsqueeze(1).to_broadcast([P, GT, E]), ALU.add))
                            if K == 1:
                                dve.tensor_reduce(top1[:], lg, AX.X, ALU.max).then_inc(topped, 1)
                                dve.wait_ge(scored, 1)
                                for t in range(GT):
                                    ins = dve.tensor_scalar(xs[:, t, :], xn[:, t, :], score[:, t:t + 1], None, ALU.mult)
                                ins.then_inc(rows_ready, 1)

                        @block.tensor
                        def _(pe):
                            pe.wait_ge(normed_ready, 1)
                            for t in range(GT):
                                for c in range(C):
                                    ins = pe.transpose(ring[:, 0, c * 512 + t * P:c * 512 + (t + 1) * P], xn[:, t, c * P:(c + 1) * P], ident[:])
                            ins.then_inc(rg.full(("xt",)), 1)
                            rg.wait_taken(pe, ("xt",))
                            for t in range(GT):
                                for c in range(C):
                                    ins = pe.matmul(acc[:, 0, t * E:(t + 1) * E], x_t[:, c, t * P:(t + 1) * P], wr[:, c, :],
                                                    start=(c == 0), stop=(c == C - 1), skip_group_check=True)
                            ins.then_inc(ac.full(("lg",)), 1)

                        @block.scalar
                        def _(act):
                            rg.wait_full(act, ("xt",))
                            act.activation(x_t[:].rearrange("p c n -> p (c n)"), ring[:, 0, :], ACT.Copy).then_inc(rg.taken(("xt",)), 1)
                            act.activation(xt_all[:, :, bass.ds(g * 512, 512)], ring[:, 0, :].rearrange("p (c n) -> p c n", c=C),
                                           ACT.Copy).then_inc(kept, 1)
                            if K == 1:
                                act.wait_ge(topped, 1)
                                act.activation(score[:], top1[:], ACT.Sigmoid).then_inc(scored, 1)

                        @block.sync
                        def _(sp):
                            sp.wait_ge(rows_ready if K == 1 else normed_ready, 1)
                            sp.dma_start(x_rows.rearrange("(g t p) d -> g p t d", t=GT, p=P)[bass.ds(g, 1)].rearrange("o p t d -> (o p) t d"),
                                         (xs if K == 1 else xn)[:]).then_inc(stored, 16)
                            sp.wait_ge(stored, 16)

                    with ExitStack() as pz:
                        top8 = s_("top8", [P, T, 8], F32, pz)
                        idx8 = s_("idx8", [P, T, 8], U32, pz)
                        idxf = s_("idxf", [P, T, 8], F32, pz)
                        e_iota = s_("e_iota", [P, E], F32, pz)
                        chosen = s_("chosen", [P, K, T, E], F32, pz)
                        pairs = s_("pairs", [P, T, E], BF16, pz)
                        before = s_("before", [P, P], BF16, pz)
                        ones = s_("ones", [P, P], BF16, pz)
                        onesf = s_("onesf", [P, max(T, E)], F32, pz)
                        count = s_("count", [P, T, E], F32, pz)
                        incl = s_("incl", [P, T, E], F32, pz)
                        pos = s_("pos", [P, T, E], F32, pz)
                        work = s_("work", [P, T, E], F32, pz)
                        padded = s_("padded", [P, 3, E], F32, pz)
                        padded_i = s_("padded_i", [P, 2, E], I32, pz)
                        slotf = s_("slotf", [P, K, T], F32, pz)
                        starts = s_("starts", [1, NB], F32, pz)
                        passed = s_("passed", [1, NB, E], F32, pz)
                        blockf = s_("blockf", [1, NB], F32, pz)
                        sums = s_("sums", [P, 4, T], F32, pz)
                        exps = s_("exps", [P, T, 8], F32, pz)
                        with Stage() as ctx:
                            linked = sem(ctx, f"{tag}r_linked")
                            consts = sem(ctx, f"{tag}r_consts")
                            pairs_ready = sem(ctx, f"{tag}r_pairs_ready")
                            ranked = sem(ctx, f"{tag}r_ranked")
                            shifted = sem(ctx, f"{tag}r_shifted")
                            exped = sem(ctx, f"{tag}r_exped")
                            block = open_block(ctx)

                            @block.gpsimd
                            def _(pool):
                                pool.iota(e_iota[:], [[1, E]], base=0, channel_multiplier=0, allow_small_or_imprecise_dtypes=True).then_inc(consts, 1)
                                pool.iota(starts[:], [[P, NB]], base=0, channel_multiplier=0, allow_small_or_imprecise_dtypes=True).then_inc(consts, 1)
                                pool.memset(ones[:], 1.0).then_inc(consts, 1)
                                pool.memset(onesf[:], 1.0).then_inc(consts, 1)
                                pool.wait_ge(consts, 4)
                                pool.affine_select(out=before[:], in_=ones[:], compare_op=ALU.is_gt, fill=0.0, base=0,
                                                   pattern=[[1, P]], channel_multiplier=-1).then_inc(consts, 1)

                            @block.tensor
                            def _(pe):
                                pe.wait_ge(consts, 5)
                                pe.wait_ge(pairs_ready, 1)
                                flat = pairs[:].rearrange("p t e -> p (t e)")
                                for n in range(0, TE, 512):
                                    m = min(512, TE - n)
                                    pe.matmul(ring[:, 0, n:n + m], before[:], flat[:, n:n + m], start=True, stop=True)
                                    ins = pe.matmul(ring[:, 1, n:n + m], ones[:], flat[:, n:n + m], start=True, stop=True)
                                ins.then_inc(ranked, 1)

                            @block.scalar
                            def _(act):
                                if K > 1:
                                    act.wait_ge(shifted, 1)
                                    act.activation(work[:], work[:], ACT.Exp)
                                    act.activation(exps[:], exps[:], ACT.Exp).then_inc(exped, 1)

                            @block.vector
                            def _(dve):
                                link = chain(dve, linked)
                                dve.wait_ge(consts, 5)
                                for t in range(T):
                                    ins = dve.max(top8[:, t, :], logits[:, t, :])
                                link(ins)
                                for t in range(T):
                                    ins = dve.max_index(idx8[:, t, :], top8[:, t, :], logits[:, t, :])
                                link(ins)
                                link(dve.tensor_copy(idxf[:], idx8[:]))
                                for k in range(K):
                                    ins = dve.tensor_tensor(chosen[:, k, :, :], e_iota[:].unsqueeze(1).to_broadcast([P, T, E]),
                                                            idxf[:, :, k:k + 1].to_broadcast([P, T, E]), ALU.is_equal)
                                link(ins)
                                if K == 1:
                                    dve.tensor_copy(pairs[:], chosen[:, 0, :, :]).then_inc(pairs_ready, 1)
                                    dve.memset(shares[:], 1.0)
                                else:
                                    link(dve.tensor_tensor(pos[:], chosen[:, 0, :, :], chosen[:, 1, :, :], ALU.add))
                                    for k in range(2, K):
                                        last = k == K - 1
                                        ins = dve.tensor_tensor(pairs[:] if last else pos[:], pos[:], chosen[:, k, :, :], ALU.add)
                                        if last:
                                            ins.then_inc(pairs_ready, 1)
                                        else:
                                            link(ins)
                                    link(dve.tensor_tensor(work[:], logits[:], top8[:, :, 0:1].to_broadcast([P, T, E]), ALU.subtract))
                                    dve.tensor_tensor(exps[:], top8[:], top8[:, :, 0:1].to_broadcast([P, T, 8]), ALU.subtract).then_inc(shifted, 1)
                                    dve.wait_ge(exped, 1)
                                    link(dve.tensor_reduce(sums[:, 0, :], work[:], AX.X, ALU.add))
                                    link(dve.reciprocal(sums[:, 1, :], sums[:, 0, :]))
                                    link(dve.tensor_tensor(exps[:, :, 0:K], exps[:, :, 0:K], sums[:, 1, :].unsqueeze(2).to_broadcast([P, T, K]), ALU.mult))
                                    link(dve.tensor_reduce(sums[:, 2, :], exps[:, :, 0:K], AX.X, ALU.add))
                                    link(dve.tensor_scalar(sums[:, 2, :], sums[:, 2, :], 1e-12, None, ALU.max))
                                    link(dve.reciprocal(sums[:, 3, :], sums[:, 2, :]))
                                    for k in range(K):
                                        ins = dve.tensor_tensor(shares[:, k, :], exps[:, :, k], sums[:, 3, :], ALU.mult)
                                link(ins) if K > 1 else None
                                dve.wait_ge(ranked, 1)
                                link(dve.tensor_copy(count[:].rearrange("p t e -> p (t e)"), ring[:, 1, 0:TE]))
                                dve.tensor_copy(pos[:].rearrange("p t e -> p (t e)"), ring[:, 0, 0:TE])
                                for e in range(E):
                                    ins = dve.tensor_tensor_scan(incl[:, :, e], onesf[:, 0:T], count[:, :, e], 0.0, ALU.mult, ALU.add)
                                link(ins)
                                link(dve.tensor_scalar(padded[:, 0, :], incl[:, T - 1, :], float(P - 1), None, ALU.add))
                                link(dve.tensor_copy(padded_i[:, 0, :], padded[:, 0, :]))
                                link(dve.tensor_scalar(padded_i[:, 1, :], padded_i[:, 0, :], -P, None, ALU.bitwise_and))
                                link(dve.tensor_copy(padded[:, 0, :], padded_i[:, 1, :]))
                                link(dve.tensor_tensor_scan(padded[:, 1, :], onesf[:, 0:E], padded[:, 0, :], 0.0, ALU.mult, ALU.add))
                                link(dve.tensor_tensor(padded[:, 2, :], padded[:, 1, :], padded[:, 0, :], ALU.subtract))
                                link(dve.tensor_tensor(work[:], incl[:], count[:], ALU.subtract))
                                link(dve.tensor_tensor(pos[:], pos[:], work[:], ALU.add))
                                link(dve.tensor_tensor(pos[:], pos[:], padded[:, 2, :].unsqueeze(1).to_broadcast([P, T, E]), ALU.add))
                                for k in range(K):
                                    link(dve.tensor_tensor(work[:], pos[:], chosen[:, k, :, :], ALU.mult))
                                    link(dve.tensor_reduce(slotf[:, k, :], work[:], AX.X, ALU.add))
                                dve.tensor_copy(slots[:], slotf[:])
                                link(dve.tensor_scalar(shares[:], shares[:], gate, None, ALU.mult))
                                link(dve.tensor_tensor(passed[:], padded[0:1, 1, :].unsqueeze(1).to_broadcast([1, NB, E]),
                                                       starts[:].unsqueeze(2).to_broadcast([1, NB, E]), ALU.is_le))
                                link(dve.tensor_reduce(blockf[:], passed[:], AX.X, ALU.add))
                                link(dve.tensor_scalar(blockf[:], blockf[:], float(E - 1), None, ALU.min))
                                dve.tensor_copy(block_expert[:], blockf[:])

                    with ExitStack() as pz:
                        hidden = s_("hidden", [P, 4, 512], F32, pz)
                        sil = s_("sil", [P, 2, 512], F32, pz)
                        slot4 = s_("slot4", [P, K, GT], U32, pz)
                        token4 = s_("token4", [P, GT], F32, pz)
                        token_all = s_("token_all", [P, T], F32, pz)
                        with Stage() as ctx:
                            block = open_block(ctx)

                            @block.gpsimd
                            def _(pool):
                                pool.iota(token_all[:], [[P, T]], base=0, channel_multiplier=1, allow_small_or_imprecise_dtypes=True)

                        with nc.Fori(0, G) as g, Stage() as ctx:
                            rg, ac = rotations(ctx, f"{tag}s", [("gu", i) for i in range(4)], [("dn", t) for t in range(GT)])
                            linked = sem(ctx, f"{tag}s_linked")
                            silued = sem(ctx, f"{tag}s_silued")
                            picked = sem(ctx, f"{tag}s_picked")
                            placed = sem(ctx, f"{tag}s_placed")
                            block = open_block(ctx)

                            @block.gpsimd
                            def _(pool):
                                pool.wait_ge(picked, 2)
                                for t in range(GT):
                                    for k in range(K):
                                        pool.indirect_dma_start(out=token_of_slot, out_offset=bass.IndirectOffsetOnAxis(ap=slot4[:, k, t:t + 1], axis=0),
                                                                in_=token4[:, t:t + 1], in_offset=None).then_inc(placed, 16)
                                pool.wait_ge(placed, 16 * GT * K)

                            @block.tensor
                            def _(pe):
                                for i in range(4):
                                    rg.wait_room(pe, ("gu", i))
                                    for j in range(2):
                                        for c in range(C):
                                            ins = pe.matmul(ring[:, rg.slot(("gu", i)), 512 * j:512 * j + 512],
                                                            ws[:, 1024 * j + 512 * c + P * i:1024 * j + 512 * c + P * i + P],
                                                            xt_all[:, c, bass.ds(g * 512, 512)], start=(c == 0), stop=(c == C - 1))
                                    ins.then_inc(rg.full(("gu", i)), 1)
                                for i in range(4):
                                    rg.wait_taken(pe, ("gu", i))
                                for t in range(GT):
                                    ac.wait_room(pe, ("dn", t))
                                    for i in range(4):
                                        ins = pe.matmul(acc[:, ac.slot(("dn", t)), 0:D], hidden[:, i, t * P:(t + 1) * P],
                                                        ws[:, 2048 + D * i:2048 + D * i + D], start=(i == 0), stop=(i == 3))
                                    ins.then_inc(ac.full(("dn", t)), 1)

                            @block.scalar
                            def _(act):
                                for i in range(4):
                                    rg.wait_full(act, ("gu", i))
                                    if i >= 2:
                                        rg.wait_taken(act, ("gu", i - 2))
                                    act.activation(sil[:, i % 2, :], ring[:, rg.slot(("gu", i)), 0:512], ACT.Silu).then_inc(silued, 1)

                            @block.vector
                            def _(dve):
                                link = chain(dve, linked)
                                dve.tensor_copy(slot4[:], slots[:, :, bass.ds(g * GT, GT)]).then_inc(picked, 1)
                                dve.tensor_copy(token4[:], token_all[:, bass.ds(g * GT, GT)]).then_inc(picked, 1)
                                dve.tensor_copy(x4[:], x_all[:, bass.ds(g * GT, GT), :])
                                for i in range(4):
                                    dve.wait_ge(silued, i + 1)
                                    dve.tensor_tensor(hidden[:, i, :], sil[:, i % 2, :], ring[:, rg.slot(("gu", i)), 512:1024], ALU.mult)\
                                       .then_inc(rg.taken(("gu", i)), 1)
                                rg.wait_taken(dve, ("gu", 3))
                                for t in range(GT):
                                    ac.wait_full(dve, ("dn", t))
                                    dve.scalar_tensor_tensor(out=x4[:, t, :], in0=acc[:, ac.slot(("dn", t)), 0:D], scalar=gate, in1=x4[:, t, :],
                                                             op0=ALU.mult, op1=ALU.add).then_inc(ac.taken(("dn", t)), 1)
                                for t in range(GT):
                                    ac.wait_taken(dve, ("dn", t))
                                dve.tensor_copy(x_all[:, bass.ds(g * GT, GT), :], x4[:])

                with ExitStack() as pz:
                    halves = [(n, min(P, NB - n)) for n in range(0, NB, P)]
                    by_block = s_("by_block", [P, len(halves), P], F32, pz)
                    with Stage() as ctx:
                        loaded = sem(ctx, f"{tag}t_loaded")
                        turned = sem(ctx, f"{tag}t_turned")
                        block = open_block(ctx)

                        @block.sync
                        def _(sp):
                            for i, (n, m) in enumerate(halves):
                                sp.dma_start(by_block[0:m, i, :], token_of_slot.rearrange("(b p) o -> b (p o)", p=P)[n:n + m, :]).then_inc(loaded, 16)

                        @block.tensor
                        def _(pe):
                            pe.wait_ge(loaded, 16 * len(halves))
                            for i, (n, m) in enumerate(halves):
                                ins = pe.transpose(ring[:, 0, n:n + m], by_block[0:m, i, :], ident[0:m, 0:m])
                            ins.then_inc(turned, 1)

                        @block.vector
                        def _(dve):
                            dve.wait_ge(turned, 1)
                            dve.tensor_copy(token_idx[:], ring[:, 0, 0:NB])

                with ExitStack() as pz:
                    WN = w_experts.shape[2]
                    U = per_turn
                    WB = 4 if K == 1 else 8
                    XB = 4
                    we = s_("we", [P, WB, WN], F32, pz)
                    xg = s_("xg", [P, XB, D], F32, pz)
                    xgt = s_("xgt", [P, 2, C, P], F32, pz)
                    sil = s_("esil", [P, 2, HW], F32, pz)
                    hid = s_("hid", [P, 2, HW], F32, pz)
                    yb = s_("yb", [P, XB, D], F32, pz)
                    turn_idx = s_("turn_idx", [P, U], U32, pz)
                    UP = 512 if I > 1 else HW
                    ring_order = [("x", 0)]
                    for u in range(U):
                        ring_order += [("x", u + 1)] * (u + 1 < U) + [("gu", u)]
                    with nc.Fori(0, turns) as turn, Stage() as ctx:
                        rg, ac = rotations(ctx, f"{tag}e", ring_order, [("y", u) for u in range(U)])
                        picked = sem(ctx, f"{tag}e_picked")
                        weighted = [sem(ctx, f"{tag}e_weights{i}") for i in range(WB)]
                        gathered = [sem(ctx, f"{tag}e_gathered{i}") for i in range(XB)]
                        stored = [sem(ctx, f"{tag}e_stored{i}") for i in range(XB)]
                        silued = sem(ctx, f"{tag}e_silued")
                        block = open_block(ctx)

                        @block.sync
                        def _(sp):
                            for u in range(U):
                                e = sp.value_load(block_expert[0:1, bass.ds(turn * U + u, 1)], min_val=0, max_val=E - 1)
                                if u >= WB:
                                    ac.wait_full(sp, ("y", u - WB))
                                sp.dma_start(we[:, u % WB, :], w_experts[bass.ds(e, 1), :, :].rearrange("o p n -> (o p) n")).then_inc(weighted[u % WB], 16)

                        @block.gpsimd
                        def _(pool):
                            pool.wait_ge(picked, 1)
                            for u in range(U):
                                if u >= XB:
                                    rg.wait_full(pool, ("x", u - XB))
                                pool.indirect_dma_start(out=xg[:, u % XB, :], out_offset=None, in_=x_rows,
                                                        in_offset=bass.IndirectOffsetOnAxis(ap=turn_idx[:, u:u + 1], axis=0)).then_inc(gathered[u % XB], 16)
                            for i in range(XB):
                                pool.wait_ge(gathered[i], 16 * ((U - 1 - i) // XB + 1))

                        @block.tensor
                        def _(pe):
                            def rows(u):
                                pe.wait_ge(gathered[u % XB], 16 * (u // XB + 1))
                                rg.wait_room(pe, ("x", u))
                                for c in range(C):
                                    ins = pe.transpose(ring[:, rg.slot(("x", u)), c * P:(c + 1) * P], xg[:, u % XB, c * P:(c + 1) * P], ident[:])
                                ins.then_inc(rg.full(("x", u)), 1)

                            def gate_up(u):
                                rg.wait_taken(pe, ("x", u))
                                pe.wait_ge(weighted[u % WB], 16 * (u // WB + 1))
                                rg.wait_room(pe, ("gu", u))
                                for j in range(2):
                                    for i in range(I):
                                        for c in range(C):
                                            w0 = C * HW * j + HW * c + P * i
                                            ins = pe.matmul(ring[:, rg.slot(("gu", u)), UP * j + P * i:UP * j + P * i + P], we[:, u % WB, w0:w0 + P],
                                                            xgt[:, u % 2, c, :], start=(c == 0), stop=(c == C - 1), skip_group_check=True)
                                ins.then_inc(rg.full(("gu", u)), 1)

                            def down(u):
                                rg.wait_taken(pe, ("gu", u))
                                ac.wait_room(pe, ("y", u))
                                for i in range(I):
                                    w0 = 2 * C * HW + D * i
                                    ins = pe.matmul(acc[:, ac.slot(("y", u)), 0:D], hid[:, u % 2, P * i:P * i + P], we[:, u % WB, w0:w0 + D],
                                                    start=(i == 0), stop=(i == I - 1))
                                ins.then_inc(ac.full(("y", u)), 1)

                            rows(0)
                            for u in range(U):
                                if u + 1 < U:
                                    rows(u + 1)
                                gate_up(u)
                                if u >= 1:
                                    down(u - 1)
                            down(U - 1)

                        def put_rows(act, u):
                            ac.wait_full(act, ("y", u))
                            if u >= XB:
                                act.wait_ge(stored[u % XB], 16 * (u // XB))
                            act.activation(yb[:, u % XB, :], acc[:, ac.slot(("y", u)), 0:D], ACT.Copy).then_inc(ac.taken(("y", u)), 1)
                            ac.wait_taken(act, ("y", u))
                            act.dma_start(y_rows.rearrange("(b p) d -> b p d", p=P)[bass.ds(turn * U + u, 1)].rearrange("o p d -> (o p) d"),
                                          yb[:, u % XB, :]).then_inc(stored[u % XB], 16)
                            if u == U - 1:
                                for i in range(min(XB, U)):
                                    act.wait_ge(stored[i], 16 * ((U - 1 - i) // XB + 1))

                        @block.scalar
                        def _(act):
                            for u in range(U):
                                rg.wait_full(act, ("gu", u))
                                if u >= 2:
                                    rg.wait_taken(act, ("gu", u - 2))
                                act.activation(sil[:, u % 2, :], ring[:, rg.slot(("gu", u)), 0:HW], ACT.Silu).then_inc(silued, 1)
                                if u >= 1:
                                    put_rows(act, u - 1)
                            put_rows(act, U - 1)

                        @block.vector
                        def _(dve):
                            dve.tensor_copy(turn_idx[:], token_idx[:, bass.ds(turn * U, U)]).then_inc(picked, 1)

                            def rows(u):
                                rg.wait_full(dve, ("x", u))
                                if u >= 2:
                                    rg.wait_full(dve, ("gu", u - 2))
                                dve.tensor_copy(xgt[:, u % 2, :, :].rearrange("p c n -> p (c n)"), ring[:, rg.slot(("x", u)), 0:D])\
                                   .then_inc(rg.taken(("x", u)), 1)

                            rows(0)
                            for u in range(U):
                                if u + 1 < U:
                                    rows(u + 1)
                                dve.wait_ge(silued, u + 1)
                                if u >= 2:
                                    ac.wait_full(dve, ("y", u - 2))
                                dve.tensor_tensor(hid[:, u % 2, :], sil[:, u % 2, :], ring[:, rg.slot(("gu", u)), UP:UP + HW], ALU.mult)\
                                   .then_inc(rg.taken(("gu", u)), 1)

                with ExitStack() as pz:
                    CT = 8 if T % 8 == 0 else GT
                    YB = 8
                    xc = s_("xc", [P, CT, D], F32, pz)
                    yk = s_("yk", [P, YB, D], F32, pz)
                    slot_c = s_("slot_c", [P, K, CT], U32, pz)
                    share_c = s_("share_c", [P, K, CT], F32, pz)
                    with nc.Fori(0, T // CT) as g, Stage() as ctx:
                        picked = sem(ctx, f"{tag}c_picked")
                        gathered = [sem(ctx, f"{tag}c_gathered{i}") for i in range(YB)]
                        linked = sem(ctx, f"{tag}c_linked")
                        added = sem(ctx, f"{tag}c_added")
                        block = open_block(ctx)

                        @block.gpsimd
                        def _(pool):
                            pool.wait_ge(picked, 1)
                            for n in range(CT * K):
                                k, t = n // CT, n % CT
                                if n >= YB:
                                    pool.wait_ge(added, n - YB + 1)
                                pool.indirect_dma_start(out=yk[:, n % YB, :], out_offset=None, in_=y_rows,
                                                        in_offset=bass.IndirectOffsetOnAxis(ap=slot_c[:, k, t:t + 1], axis=0)).then_inc(gathered[n % YB], 16)
                            for i in range(min(YB, CT * K)):
                                pool.wait_ge(gathered[i], 16 * ((CT * K - 1 - i) // YB + 1))

                        @block.vector
                        def _(dve):
                            link = chain(dve, linked)
                            dve.tensor_copy(slot_c[:], slots[:, :, bass.ds(g * CT, CT)]).then_inc(picked, 1)
                            dve.tensor_copy(share_c[:], shares[:, :, bass.ds(g * CT, CT)])
                            link(dve.tensor_copy(xc[:], x_all[:, bass.ds(g * CT, CT), :]))
                            for n in range(CT * K):
                                k, t = n // CT, n % CT
                                dve.wait_ge(gathered[n % YB], 16 * (n // YB + 1))
                                if n >= CT:
                                    dve.wait_ge(added, n - CT + 1)
                                dve.scalar_tensor_tensor(out=xc[:, t, :], in0=yk[:, n % YB, :], scalar=share_c[:, k, t:t + 1], in1=xc[:, t, :],
                                                         op0=ALU.mult, op1=ALU.add).then_inc(added, 1)
                            dve.wait_ge(added, CT * K)
                            dve.tensor_copy(x_all[:, bass.ds(g * CT, CT), :], xc[:])

        if "B" in stages:
            expert_layer("b", 1, 512, gates[:, 5:6], a["L1_ffn_gate_w"], None, a["shared1"], a["experts1"])


        if "C" in stages:
            with ExitStack() as ph:
                xb = sb(ph, "c_xb", [P, 2, D])
                cb = sb(ph, "c_cb", [P, 2, D])
                normed = sb(ph, "c_normed", [P, 2, D])
                feats = sb(ph, "c_feats", [P, 8, 256])
                d_t = sb(ph, "c_d_t", [P, C, 256])
                qs_t = sb(ph, "c_qs_t", [P, C, 256])
                attn = sb(ph, "c_attn", [P, 2, 256])
                attn_t = sb(ph, "c_attn_t", [P, 2, 256])
                cols = sb(ph, "c_cols", [P, 16])
                srow = sb(ph, "c_srow", [1, 2, 256])
                sums = sb(ph, "c_sums", [1, 4])
                one = sb(ph, "c_one", [1, 2])
                sim_cols = sb(ph, "c_sim_cols", [P, 3, C])
                b_sim = sb(ph, "c_b_sim", [P, 1])
                wqv = sb(ph, "c_wqv", [P, 8, D])
                rows = sb(ph, "c_rows", [P, 3, D])
                win = sb(ph, "c_win", [P, C, 64])
                in_col = sb(ph, "c_in_col", [64, 2])
                bd1 = sb(ph, "c_bd1", [64, 8 * P])
                b1_cols = sb(ph, "c_b1_cols", [P, 8])
                bd2 = sb(ph, "c_bd2", [P, 8, 64])
                wo2 = sb(ph, "c_wo2", [64, D])
                s_t = sb(ph, "c_s_t", [64, 256])
                g_t = sb(ph, "c_g_t", [64, 256])
                h_t = sb(ph, "c_h_t", [P, 8, 256])
                w3 = sb(ph, "c_w3", [P, C, D])
                mask_i = sb(ph, "c_mask_i", [P, 2, 256], I32)
                neg_mask = sb(ph, "c_neg_mask", [P, 2, 256])
                neg_mask_t = sb(ph, "c_neg_mask_t", [P, 2, 256], BF16)
                ident_bf = sb(ph, "c_ident_bf", [P, P], BF16)
                inv = sb(ph, "c_inv", [P, 2, HEADS])
                heads = sb(ph, "c_heads", [P, 2, 256])
                heads_t = sb(ph, "c_heads_t", [P, C, 256])
                x_t = sb(ph, "c_x_t", [P, C, 256])
                q_pad = sb(ph, "c_q_pad", [P, 2, HEADS, SLOT])
                v_pad = sb(ph, "c_v_pad", [P, 2, HEADS, SLOT])
                q_t = sb(ph, "c_q_t", [P, 4, 4, 256])
                k_t = sb(ph, "c_k_t", [P, 4, 256])
                probs = sb(ph, "c_probs", [P, 3, 2, 2, 256])
                junk = sb(ph, "c_junk", [P, 8, 256])

                with Stage() as ctx:
                    loaded = sem(ctx, "c_loaded")
                    made = sem(ctx, "c_made")
                    masked = sem(ctx, "c_masked")
                    turned = sem(ctx, "c_turned")
                    block = open_block(ctx)
                    loads = [
                        (mask_i[:], a["mask_qk"].rearrange("(t p) k -> p t k", p=P)),
                        (sim_cols[:], a["sim_cols"].rearrange("p (w c) -> p w c", w=3)),
                        (b_sim[:], every("L2_xattn_b_sim")),
                        (wqv[:], a["L2_xattn_W_qv"].rearrange("(c p) n -> p c n", p=P)),
                        (rows[:, 0, :], every("L2_xattn_b_qv")), (rows[:, 1, :], every("L2_ffn_bout")),
                        (rows[:, 2, :], every("L3_xattn_b_out")),
                        (win[:], a["L2_ffn_Win"].rearrange("(c p) n -> p c n", p=P)),
                        (in_col[:], a["in_col"]), (bd1[:], a["bd1"]), (b1_cols[:], a["b1_cols"]),
                        (bd2[:], a["bd2"].rearrange("(c p) n -> p c n", p=P)),
                        (wo2[:], a["L2_ffn_Wout"]),
                        (w3[:], a["w3_t"].rearrange("(c p) n -> p c n", p=P)),
                    ]

                    @block.sync
                    def _(sp):
                        for dst, src in loads:
                            sp.dma_start(dst, src).then_inc(loaded, 16)
                        sp.wait_ge(loaded, 16 * len(loads))

                    @block.gpsimd
                    def _(pool):
                        pool.memset(q_pad[:], 0.0).then_inc(made, 1)
                        pool.memset(v_pad[:], 1.0).then_inc(made, 1)
                        pool.memset(one[:], 1.0).then_inc(made, 1)
                        pool.tensor_copy(ident_bf[:], ident[:]).then_inc(made, 1)
                        pool.wait_ge(made, 4)

                    @block.vector
                    def _(dve):
                        dve.wait_ge(loaded, 16 * len(loads))
                        dve.tensor_scalar(neg_mask[:], mask_i[:], 0.0, -BIG, ALU.is_equal, ALU.mult).then_inc(masked, 1)
                        for i, g in enumerate((2, 6, 3)):
                            dve.tensor_scalar(rows[:, i, :], rows[:, i, :], gates[:, g:g + 1], None, ALU.mult)
                        dve.wait_ge(turned, 1)
                        dve.tensor_copy(neg_mask_t[:].rearrange("p k n -> p (k n)"), ring[:, 0, 0:512])

                    @block.tensor
                    def _(pe):
                        pe.wait_ge(masked, 1)
                        for k in range(2):
                            for t in range(2):
                                ins = pe.transpose(ring[:, 0, 256 * k + P * t:256 * k + P * t + P], neg_mask[:, t, k * P:(k + 1) * P], ident[:])
                        ins.then_inc(turned, 1)

                ring_order = [("hd",), ("cT",), ("sim",), ("AT",), ("hq",), ("bcol",), ("hbar",), ("gT",), ("s",), ("h", 0), ("h", 1), ("g",)]
                ring_order += narrow_order("c") + [("cHT",)]
                acc_order = [(n, t) for n in ("qv", "fo") for t in range(2)]
                acc_order += [("c", "av", t) for t in range(2)] + [("cp", t) for t in range(2)]

                norm_first_batch("c", normed[:], 1)
                with nc.Fori(0, B) as b, Stage() as ctx:
                    rg, ac = rotations(ctx, "c", ring_order, acc_order)
                    linked = sem(ctx, "c_dve_linked")
                    root_asked = sem(ctx, "c_root_asked")
                    root_given = sem(ctx, "c_root_given")
                    context_loaded = sem(ctx, "c_context_loaded")
                    normed_ready = sem(ctx, "c_normed_ready")
                    queries_ready = sem(ctx, "c_queries_ready")
                    weights_used = sem(ctx, "c_weights_used")
                    sim_ready = sem(ctx, "c_sim_ready")
                    exps = sem(ctx, "c_exps")
                    soft = sem(ctx, "c_soft")
                    block = open_block(ctx)
                    w = dict(q_pad=q_pad, q_t=q_t, k_t=k_t, v_pad=v_pad, probs=probs, inv=inv, heads=heads, weights_used=weights_used,
                             weights_base=0, neg_mask=neg_mask, neg_mask_t=neg_mask_t, ident_bf=ident_bf, junk=junk)

                    @block.tensor
                    def _(pe):
                        s = rg.slot(("hd",))
                        rg.wait_room(pe, ("hd",))
                        for i, src in enumerate((normed, cb)):
                            if i == 1:
                                pe.wait_ge(context_loaded, 16)
                            for t in range(2):
                                for c in range(C):
                                    ins = pe.transpose(ring[:, s, 512 * i + 256 * c + P * t:512 * i + 256 * c + P * t + P],
                                                       src[:, t, c * P:(c + 1) * P], ident[:])
                        ins.then_inc(rg.full(("hd",)), 1)
                        pe.wait_ge(queries_ready, 1)
                        rg.wait_room(pe, ("cT",))
                        for g in range(4):
                            for t in range(2):
                                ins = pe.transpose(ring[:, rg.slot(("cT",)), 256 * g + P * t:256 * g + P * t + P],
                                                   v_pad[:, t, 4 * g:4 * g + 4, :].rearrange("p h s -> p (h s)"), ident[:])
                        ins.then_inc(rg.full(("cT",)), 1)
                        pe.wait_ge(sim_ready, 1)
                        rg.wait_room(pe, ("sim",))
                        s = rg.slot(("sim",))
                        for t in range(2):
                            for c in range(C):
                                pe.matmul(ring[:, s, 256 * t:256 * t + 256], qs_t[:, c, t * P:(t + 1) * P], d_t[:, c, :],
                                          start=(c == 0), stop=(c == C - 1), skip_group_check=True)
                        for t in range(2):
                            for c in range(C):
                                ins = pe.matmul(ring[:, s, 512 + t:513 + t], feats[:, c, t * P:(t + 1) * P], sim_cols[:, 0, c:c + 1],
                                                start=(c == 0), stop=(c == C - 1), skip_group_check=True)
                        ins.then_inc(rg.full(("sim",)), 1)
                        pe.wait_ge(sim_ready, 3)
                        rg.wait_room(pe, ("AT",))
                        s = rg.slot(("AT",))
                        for k in range(2):
                            for t in range(2):
                                pe.transpose(ring[:, s, 256 * k + P * t:256 * k + P * t + P], attn[:, t, k * P:(k + 1) * P], ident[:])
                        for t in range(2):
                            ins = pe.matmul(ring[0:1, s, 512 + P * t:512 + P * t + P], cols[:, 4 + t:5 + t], ident[:], start=True, stop=True,
                                            skip_group_check=True)
                        ins.then_inc(rg.full(("AT",)), 1)
                        pe.wait_ge(exps, 2)
                        rg.wait_room(pe, ("hq",))
                        for c in range(C):
                            for k in range(2):
                                ins = pe.matmul(ring[:, rg.slot(("hq",)), 256 * c:256 * c + 256], cb[:, k, c * P:(c + 1) * P], attn_t[:, k, :],
                                                start=(k == 0), stop=(k == 1), skip_group_check=True)
                        ins.then_inc(rg.full(("hq",)), 1)
                        pe.wait_ge(sim_ready, 5)
                        rg.wait_room(pe, ("bcol",))
                        for t in range(2):
                            ins = pe.matmul(ring[:, rg.slot(("bcol",)), t:t + 1], srow[0:1, 1, t * P:(t + 1) * P], one[0:1, 0:1], start=True, stop=True,
                                            skip_group_check=True)
                        ins.then_inc(rg.full(("bcol",)), 1)
                        rg.wait_taken(pe, ("bcol",))
                        rg.wait_room(pe, ("hbar",))
                        for c in range(C):
                            for t in range(2):
                                ins = pe.matmul(ring[:, rg.slot(("hbar",)), c:c + 1], normed[:, t, c * P:(c + 1) * P], cols[:, 8 + t:9 + t],
                                                start=(t == 0), stop=(t == 1), skip_group_check=True)
                        ins.then_inc(rg.full(("hbar",)), 1)
                        pe.wait_ge(sim_ready, 6)
                        for t in range(2):
                            ac.wait_room(pe, ("qv", t))
                            for j in range(8):
                                ins = pe.matmul(acc[:, ac.slot(("qv", t)), 0:D], feats[:, j, t * P:(t + 1) * P], wqv[:, j, :],
                                                start=(j == 0), stop=(j == 7))
                            ins.then_inc(ac.full(("qv", t)), 1)

                        pe.wait_ge(normed_ready, 1)
                        transpose_tiles(pe, rg, ("gT",), normed)
                        rg.wait_taken(pe, ("gT",))
                        rg.wait_room(pe, ("s",))
                        for c in range(C):
                            ins = pe.matmul(ring[0:64, rg.slot(("s",)), 0:256], win[:, c, :], x_t[:, c, :], start=(c == 0), stop=(c == C - 1))
                        ins.then_inc(rg.full(("s",)), 1)
                        rg.wait_taken(pe, ("s",))
                        for i in range(2):
                            rg.wait_room(pe, ("h", i))
                            for j in range(4):
                                ins = pe.matmul(ring[:, rg.slot(("h", i)), 256 * j:256 * j + 256], bd1[:, (4 * i + j) * P:(4 * i + j + 1) * P], s_t[:],
                                                start=True, stop=True, skip_group_check=True)
                            ins.then_inc(rg.full(("h", i)), 1)
                        rg.wait_room(pe, ("g",))
                        for i in range(2):
                            rg.wait_taken(pe, ("h", i))
                            for j in range(4):
                                ins = pe.matmul(ring[0:64, rg.slot(("g",)), 0:256], bd2[:, 4 * i + j, :], h_t[:, 4 * i + j, :],
                                                start=(i + j == 0), stop=(i == 1 and j == 3))
                        ins.then_inc(rg.full(("g",)), 1)
                        rg.wait_taken(pe, ("g",))
                        for t in range(2):
                            ac.wait_room(pe, ("fo", t))
                            pe.matmul(acc[:, ac.slot(("fo", t)), 0:D], g_t[:, t * P:(t + 1) * P], wo2[:], start=True, stop=True)\
                              .then_inc(ac.full(("fo", t)), 1)

                        rg.wait_taken(pe, ("cT",))
                        narrow_pe(pe, rg, ac, "c", w, lambda: pe.wait_ge(queries_ready, 2), lambda: None)
                        for t in range(2):
                            ac.wait_taken(pe, ("c", "av", t))
                        transpose_tiles(pe, rg, ("cHT",), heads)
                        rg.wait_taken(pe, ("cHT",))
                        project(pe, ac, "cp", heads_t, w3)

                    @block.scalar
                    def _(act):
                        def copy_tiles(name, dst):
                            rg.wait_full(act, name)
                            act.activation(dst, ring[:, rg.slot(name), 0:512].rearrange("p (c n) -> p c n", c=2),
                                           ACT.Copy).then_inc(rg.taken(name), 1)

                        rg.wait_full(act, ("hd",))
                        act.activation(feats[:, 0:2, :], ring[:, rg.slot(("hd",)), 0:512].rearrange("p (c n) -> p c n", c=2), ACT.Copy)
                        act.activation(d_t[:], ring[:, rg.slot(("hd",)), 512:1024].rearrange("p (c n) -> p c n", c=2),
                                       ACT.Copy).then_inc(rg.taken(("hd",)), 1)
                        rg.wait_full(act, ("cT",))
                        act.activation(k_t[:].rearrange("p g n -> p (g n)"), ring[:, rg.slot(("cT",)), :], ACT.Copy).then_inc(rg.taken(("cT",)), 1)
                        act.wait_ge(sim_ready, 2)
                        for t in range(2):
                            ins = act.activation(attn[:, t, :], ring[:, rg.slot(("sim",)), 256 * t:256 * t + 256], ACT.Exp,
                                                 bias=cols[:, t:t + 1], accum_out=cols[:, 2 + t:3 + t])
                        ins.then_inc(exps, 1)
                        rg.wait_full(act, ("AT",))
                        act.activation(attn_t[:], ring[:, rg.slot(("AT",)), 0:512].rearrange("p (c n) -> p c n", c=2), ACT.Copy).then_inc(exps, 1)
                        act.wait_ge(sim_ready, 4)
                        act.activation(srow[0:1, 0, :], ring[0:1, rg.slot(("AT",)), 512:768], ACT.Exp, bias=sums[0:1, 0:1],
                                       accum_out=sums[0:1, 1:2]).then_inc(soft, 1)
                        act.wait_ge(soft, 1)
                        act.wait_ge(exps, 2)
                        act.activation(sums[0:1, 3:4], sums[0:1, 1:2], ACT.Copy).then_inc(rg.taken(("AT",)), 1)
                        copy_tiles(("hq",), feats[:, 2:4, :])
                        rg.wait_full(act, ("bcol",))
                        act.activation(cols[:, 8:10], ring[:, rg.slot(("bcol",)), 0:2], ACT.Copy).then_inc(rg.taken(("bcol",)), 1)
                        rg.wait_full(act, ("hbar",))
                        act.activation(cols[:, 10:12], ring[:, rg.slot(("hbar",)), 0:2], ACT.Copy).then_inc(rg.taken(("hbar",)), 1)
                        copy_tiles(("gT",), x_t[:])
                        rg.wait_full(act, ("s",))
                        act.activation(s_t[:], ring[0:64, rg.slot(("s",)), 0:256], ACT.Identity, bias=in_col[:, 0:1]).then_inc(rg.taken(("s",)), 1)
                        for i in range(2):
                            rg.wait_full(act, ("h", i))
                            for j in range(4):
                                ins = act.activation(h_t[:, 4 * i + j, :], ring[:, rg.slot(("h", i)), 256 * j:256 * j + 256], ACT.Relu,
                                                     bias=b1_cols[:, 4 * i + j:4 * i + j + 1])
                            ins.then_inc(rg.taken(("h", i)), 1)
                        rg.wait_full(act, ("g",))
                        act.activation(g_t[:], ring[0:64, rg.slot(("g",)), 0:256], ACT.Identity, bias=in_col[:, 1:2]).then_inc(rg.taken(("g",)), 1)
                        narrow_act(act, rg, "c", w, D ** -0.5)
                        copy_tiles(("cHT",), heads_t[:])

                    @block.sync
                    def _(sp):
                        sp.dma_start(cb[:], a["ctx_1024"].rearrange("b (t p) d -> b p t d", p=P)[bass.ds(b, 1)].rearrange("o p t d -> (o p) t d"))\
                          .then_inc(context_loaded, 16)

                    @block.gpsimd
                    def _(pool):
                        roots(pool, [2, 2, 2], root_asked, root_given)

                    @block.vector
                    def _(dve):
                        link = chain(dve, linked, root_asked, root_given)
                        link(dve.tensor_copy(xb[:], x_all[:, bass.ds(b * 2, 2), :]))
                        dve.wait_ge(context_loaded, 16)
                        for t in range(2):
                            ins = dve.tensor_copy(v_pad[:, t, :, 0:HD], cb[:, t, :].rearrange("p (h n) -> p h n", n=HD))
                        ins.then_inc(queries_ready, 1)
                        rg.wait_taken(dve, ("hd",))
                        for c in range(C):
                            ins = dve.tensor_scalar(qs_t[:, c, :], feats[:, c, :], sim_cols[:, 2, c:c + 1], sim_cols[:, 1, c:c + 1], ALU.mult, ALU.add)
                        ins.then_inc(sim_ready, 1)
                        rg.wait_full(dve, ("sim",))
                        s = rg.slot(("sim",))
                        dve.tensor_reduce(cols[:, 0:2], ring[:, s, 0:512].rearrange("p (t n) -> p t n", t=2), AX.X, ALU.max, negate=True)\
                           .then_inc(sim_ready, 1)
                        dve.wait_ge(sim_ready, 2)
                        link(dve.tensor_tensor(cols[:, 6:8], ring[:, s, 512:514], cols[:, 0:2], ALU.subtract))
                        link(dve.tensor_scalar(cols[:, 4:6], cols[:, 6:8], b_sim[:, 0:1], None, ALU.add))
                        dve.wait_ge(exps, 1)
                        link(dve.reciprocal(inv[:, 0, 0:2], cols[:, 2:4]))
                        for t in range(2):
                            ins = dve.tensor_scalar(attn[:, t, :], attn[:, t, :], inv[:, 0, t:t + 1], None, ALU.mult)
                        link(ins)
                        dve.engine_nop().then_inc(sim_ready, 1)
                        dve.engine_nop().then_inc(rg.taken(("sim",)), 1)
                        rg.wait_full(dve, ("AT",))
                        dve.wait_ge(exps, 2)
                        dve.tensor_reduce(sums[0:1, 0:1], ring[0:1, rg.slot(("AT",)), 512:768], AX.X, ALU.max, negate=True).then_inc(sim_ready, 1)
                        dve.wait_ge(soft, 1)
                        link(dve.reciprocal(sums[0:1, 2:3], sums[0:1, 1:2]))
                        dve.tensor_scalar(srow[0:1, 1, :], srow[0:1, 0, :], sums[0:1, 2:3], None, ALU.mult).then_inc(sim_ready, 1)
                        rg.wait_taken(dve, ("hq",))
                        dve.tensor_tensor(feats[:, 4:6, :], feats[:, 0:2, :], feats[:, 2:4, :], ALU.mult)
                        rg.wait_taken(dve, ("hbar",))
                        for c in range(C):
                            ins = dve.tensor_scalar(feats[:, 6 + c, :], feats[:, c, :], cols[:, 10 + c:11 + c], None, ALU.mult)
                        ins.then_inc(sim_ready, 1)
                        add_projection(dve, link, ac, "qv", xb, gates[:, 2:3], rows[:, 0, :])

                        norm_tiles(dve, link, lambda t: xb[:, t, :], lambda t: normed[:, t, :])
                        dve.engine_nop().then_inc(normed_ready, 1)
                        add_projection(dve, link, ac, "fo", xb, gates[:, 6:7], rows[:, 1, :])

                        dve.memset(q_pad[:, :, :, HD:HD + 1], 0.0)
                        norm_tiles(dve, link, lambda t: xb[:, t, :], lambda t: normed[:, t, :])
                        for t in range(2):
                            ins = dve.tensor_copy(q_pad[:, t, :, 0:HD], normed[:, t, :].rearrange("p (h n) -> p h n", n=HD))
                        ins.then_inc(queries_ready, 1)
                        dve.wait_ge(queries_ready, 2)
                        narrow_maxima(dve, rg, "c", w)
                        norm_batch(dve, link, b * 2 + 2, normed[:], 1)
                        narrow_heads(dve, link, ac, "c", w)
                        add_projection(dve, link, ac, "cp", xb, gates[:, 3:4], rows[:, 2, :])
                        dve.tensor_copy(x_all[:, bass.ds(b * 2, 2), :], xb[:])


        if "D" in stages:
            expert_layer("d", 4, 128, gates[:, 7:8], a["route3"], a["L3_ffn_router_bias"], a["shared3"], a["experts3"])

        with Stage() as ctx:
            stored = sem(ctx, "stored")
            block = open_block(ctx)

            @block.sync
            def _(sp):
                sp.dma_start(out.rearrange("b (t p) d -> p (b t) d", p=P), x_all[:, 0:T, :]).then_inc(stored, 16)
                sp.wait_ge(stored, 16)


STAGES = "ABCD"


def lay_out(v):
    import numpy as np
    v = {k: np.asarray(x) for k, x in v.items()}
    d = {k: v[k] for k in ("x", "ctx_1024", "g_xattn", "g_ffn", "L0_xattn_Wq", "L0_xattn_Wkv", "L0_xattn_Wout",
                           "L0_xattn_ln_o_g", "L0_xattn_ln_o_b", "L0_ffn_bq", "L0_ffn_bv", "L0_ffn_bp",
                           "L0_ffn_br", "L0_ffn_bs", "L1_xattn_b_out", "L2_xattn_b_sim", "L2_xattn_W_qv", "L2_xattn_b_qv",
                           "L2_ffn_bout", "L2_ffn_Win", "L2_ffn_Wout", "L3_xattn_b_out", "L1_ffn_gate_w", "L3_ffn_router_bias")}

    def cols(x):
        return x.reshape(-1, P).T

    for n in ("ln_x_g", "ln_x_b", "ln_l_g", "ln_l_b"):
        d[n + "_cols"] = cols(v["L0_xattn_" + n])
    d["mask_keys"] = v["mask_BxS2_bk0"]
    d["fq_t"], d["fv_t"], d["fp_t"] = (v["L0_ffn_" + n].T for n in ("Wq", "Wv", "Wp"))
    wk = np.zeros((256, HEADS, SLOT), np.float32)
    wk[:, :, 0:HD] = v["L0_ffn_Wk"].T.reshape(256, HEADS, HD)
    d["fk_t"] = wk.reshape(256, HEADS * SLOT)
    bk = np.zeros((HEADS, SLOT), np.float32)
    bk[:, 0:HD] = v["L0_ffn_bk"].reshape(HEADS, HD)
    bk[:, HD] = 1.0
    d["fk_bias"] = bk.reshape(4, P).T
    d["frs_t"] = np.concatenate([v["L0_ffn_Wr"], v["L0_ffn_Ws"]], 0).T
    d["query_row"] = v["L0_ffn_query_embedding"].reshape(-1)
    d["temperature_row"] = v["L0_ffn_temperature"].reshape(-1)
    d["w1_t"] = v["L1_xattn_W_out"].T
    d["mask_qk"] = v["mask_1x1xSxS2_ik0"].reshape(256, 256)
    d["sim_cols"] = np.concatenate([cols(v["L2_xattn_w_sim"][256 * i:256 * i + 256]) for i in range(3)], 1)
    d["in_col"] = np.stack([v["L2_ffn_bin_"], v["L2_ffn_b2"]], 1)
    w1 = np.zeros((64, 64, 16), np.float32)
    w2 = np.zeros((64, 16, 64), np.float32)
    for m in range(64):
        w1[m, m] = v["L2_ffn_W1"][m]
        w2[m, :, m] = v["L2_ffn_W2"][m]
    d["bd1"], d["bd2"] = w1.reshape(64, 1024), w2.reshape(1024, 64)
    d["b1_cols"] = cols(v["L2_ffn_b1"].reshape(-1))
    d["w3_t"] = v["L3_xattn_w_out"].T

    def gathered_weights(gate, up, down):
        n = gate.shape[0]
        parts = [w.reshape(n, -1, P, w.shape[2]).transpose(0, 2, 1, 3).reshape(n, P, -1) for w in (gate, up, down)]
        return np.concatenate(parts, 2)

    def turned(w):
        return np.swapaxes(w, -1, -2)

    d["shared1"] = gathered_weights(*(v["L1_ffn_shared_" + n + "_w"][None] for n in ("gate", "up", "down")))[0]
    d["experts1"] = gathered_weights(*(v["L1_ffn_routed_" + n + "_w"] for n in ("gate", "up", "down")))
    d["route3"] = v["L3_ffn_router_w"].T
    d["shared3"] = gathered_weights(*(turned(v["L3_ffn_s" + n + "_w"])[None] for n in ("gate", "up", "down")))[0]
    d["experts3"] = gathered_weights(*(turned(v["L3_ffn_" + n + "_w"]) for n in ("gate", "up", "down")))
    return {k: np.ascontiguousarray(x) for k, x in d.items()}


def kernel(**inputs):
    import numpy as np
    import concourse.bacc as bacc
    from concourse.bass_utils import run_bass_kernel_spmd as run

    arrays = lay_out(inputs)
    B = arrays["x"].shape[0]
    nc = bacc.Bacc("TRN2", target_bir_lowering=False, num_devices=1)
    a = {n: nc.dram_tensor("in_" + n, x.shape, mybir.dt.from_np(x.dtype), kind="ExternalInput").ap() for n, x in arrays.items()}
    out = nc.dram_tensor("out_x", arrays["x"].shape, F32, kind="ExternalOutput").ap()
    build(nc, a, out, B, STAGES)
    r = run(nc, [{"in_" + n: x for n, x in arrays.items()}], core_ids=[0])
    return r.results[0]["out_x"]
```
